# Optimizing a Trainium2 kernel written in Bass

```python
import numpy as np
import jax
import jax.numpy as jnp

def _softmax(x, axis=-1):
    return jax.nn.softmax(x, axis=axis)

def _gelu(x):
    return jax.nn.gelu(x, approximate=True)

def _silu(x):
    return jax.nn.silu(x)

def _sigmoid(x):
    return jax.nn.sigmoid(x)

def _layernorm(x, axis=-1, eps=1e-05):
    m = jnp.mean(x, axis=axis, keepdims=True)
    v = jnp.var(x, axis=axis, keepdims=True)
    return (x - m) / jnp.sqrt(v + eps)

def _scatter_add(tgt, idx, src, axis=0):
    return tgt.at[idx].add(src)

def _segment_sum(src, seg, n):
    return jax.ops.segment_sum(src, seg, n)
kernel_name = 'mk_adaln_ffn_d2_seqx_r4_cb9d26'

def setup_inputs(seed: int=0):
    np.random.seed(seed)
    _w = jnp.asarray

    def _rec_inputs():
        import jax
        import jax.numpy as jnp
        _rk = jax.random.key(seed)
        x = 7.22e-05 + 1 * jax.random.normal(jax.random.fold_in(_rk, 1), (4, 512, 256), jnp.float32)
        _lenS = 512 - jax.random.randint(jax.random.fold_in(_rk, 7), (4,), 0, max(1, 512 // 4) + 1, jnp.int32)
        _lenS2 = 512 - jax.random.randint(jax.random.fold_in(_rk, 8), (4,), 0, max(1, 512 // 4) + 1, jnp.int32)
        cond_8 = jax.random.uniform(jax.random.fold_in(_rk, 11), (4, 8), jnp.float32, 0.0, 0.999837)
        return (x, cond_8)
    x, cond_8 = _rec_inputs()

    def _L0_cond_setup():
        import jax, jax.numpy as jnp
        import numpy as np
        key = jax.random.key(seed)
        k1, k2, k3, k4, k5 = jax.random.split(key, 5)
        B, N, T, O, G = (32, 64, 256, 256, 8)
        x = jax.random.normal(k1, (B, N, T), dtype=jnp.float32)
        y = jax.random.uniform(k2, (B, G), dtype=jnp.float32)
        weight = jax.random.normal(k3, (G, O, T), dtype=jnp.float32) * (1.0 / np.sqrt(T))
        mask = jax.random.uniform(k4, (O, T), dtype=jnp.float32)
        bias = jax.random.normal(k5, (O,), dtype=jnp.float32)
        return {'x': x, 'y': y, 'weight': weight, 'mask': mask, 'bias': bias}
    _L0_cond_all = _L0_cond_setup()
    _L0_cond_in = {k: v for k, v in _L0_cond_all.items() if k in ('weight', 'mask', 'bias')}
    del _L0_cond_all

    def _L0_ffn_setup():
        import jax, jax.numpy as jnp
        import numpy as np
        K_TOP = 2
        key = jax.random.key(seed)
        k1, k2, k3 = jax.random.split(key, 3)
        B, S, H, E = (4, 512, 256, 8)
        hidden_states = jax.random.normal(k1, (B, S, H), dtype=jnp.float32)
        router_w = jax.random.normal(k2, (E, H), dtype=jnp.float32) * 0.02
        expert_weights = jax.random.normal(k3, (E, H, H), dtype=jnp.float32) * 0.02
        return {'hidden_states': hidden_states, 'router_w': router_w, 'expert_weights': expert_weights}
    _L0_ffn_all = _L0_ffn_setup()
    _L0_ffn_in = {k: v for k, v in _L0_ffn_all.items() if k in ('router_w', 'expert_weights')}
    del _L0_ffn_all

    def _L1_cond_setup():
        import jax, jax.numpy as jnp
        import numpy as np
        R = 16
        ALPHA = 32.0
        SCALING = ALPHA / R
        key = jax.random.key(seed)
        ks = jax.random.split(key, 6)
        B, T, C, O, E = (16, 375, 256, 256, 8)
        x = jax.random.normal(ks[0], (B, T, C), dtype=jnp.float32)
        w = jax.random.uniform(ks[1], (B, E), dtype=jnp.float32)
        W_base = jax.random.normal(ks[2], (O, C), dtype=jnp.float32) * 0.02
        b_base = jax.random.normal(ks[3], (O,), dtype=jnp.float32) * 0.02
        As = jax.random.normal(ks[4], (E, R, C), dtype=jnp.float32) * 0.02
        Bs = jax.random.normal(ks[5], (E, O, R), dtype=jnp.float32) * 0.02
        return {'x': x, 'w': w, 'W_base': W_base, 'b_base': b_base, 'As': As, 'Bs': Bs}
    _L1_cond_all = _L1_cond_setup()
    _L1_cond_in = {k: v for k, v in _L1_cond_all.items() if k in ('W_base', 'b_base', 'As', 'Bs')}
    del _L1_cond_all

    def _L1_ffn_setup():
        import jax, jax.numpy as jnp
        import numpy as np
        B, L, D = (4, 512, 256)
        E, K, S = (8, 2, 2)
        F = 352
        SCALE = 1.0
        INIT = 0.02

        def _swiglu(x, wg, wu, wd):
            return jax.nn.silu(x @ wg) * (x @ wu) @ wd
        key = jax.random.key(seed)
        ks = jax.random.split(key, 8)
        return {'hidden_states': jax.random.normal(ks[0], (B, L, D), jnp.float32), 'gate_w': jax.random.normal(ks[1], (D, E), jnp.float32) * INIT, 'exp_gate': jax.random.normal(ks[2], (E, D, F), jnp.float32) * INIT, 'exp_up': jax.random.normal(ks[3], (E, D, F), jnp.float32) * INIT, 'exp_down': jax.random.normal(ks[4], (E, F, D), jnp.float32) * INIT, 'sh_gate': jax.random.normal(ks[5], (S, D, F), jnp.float32) * INIT, 'sh_up': jax.random.normal(ks[6], (S, D, F), jnp.float32) * INIT, 'sh_down': jax.random.normal(ks[7], (S, F, D), jnp.float32) * INIT}
    _L1_ffn_all = _L1_ffn_setup()
    _L1_ffn_in = {k: v for k, v in _L1_ffn_all.items() if k in ('gate_w', 'exp_gate', 'exp_up', 'exp_down', 'sh_gate', 'sh_up', 'sh_down')}
    del _L1_ffn_all
    return {'x': x, 'cond_8': cond_8, 'L0_cond_weight': _L0_cond_in['weight'], 'L0_cond_mask': _L0_cond_in['mask'], 'L0_cond_bias': _L0_cond_in['bias'], 'L0_ffn_router_w': _L0_ffn_in['router_w'], 'L0_ffn_expert_weights': _L0_ffn_in['expert_weights'], 'L1_cond_W_base': _L1_cond_in['W_base'], 'L1_cond_b_base': _L1_cond_in['b_base'], 'L1_cond_As': _L1_cond_in['As'], 'L1_cond_Bs': _L1_cond_in['Bs'], 'L1_ffn_gate_w': _L1_ffn_in['gate_w'], 'L1_ffn_exp_gate': _L1_ffn_in['exp_gate'], 'L1_ffn_exp_up': _L1_ffn_in['exp_up'], 'L1_ffn_exp_down': _L1_ffn_in['exp_down'], 'L1_ffn_sh_gate': _L1_ffn_in['sh_gate'], 'L1_ffn_sh_up': _L1_ffn_in['sh_up'], 'L1_ffn_sh_down': _L1_ffn_in['sh_down']}

def reference(x, cond_8, L0_cond_weight, L0_cond_mask, L0_cond_bias, L0_ffn_router_w, L0_ffn_expert_weights, L1_cond_W_base, L1_cond_b_base, L1_cond_As, L1_cond_Bs, L1_ffn_gate_w, L1_ffn_exp_gate, L1_ffn_exp_up, L1_ffn_exp_down, L1_ffn_sh_gate, L1_ffn_sh_up, L1_ffn_sh_down):
    import jax
    import jax.numpy as jnp

    def _L0_cond_ref(x, y, weight, mask, bias):
        import jax, jax.numpy as jnp
        import numpy as np
        masked_w = weight * mask[None, :, :]
        w_bot = jnp.einsum('bg,got->bot', y, masked_w)
        return jnp.einsum('bnt,bot->bno', x, w_bot) + bias

    def _L0_ffn_ref(hidden_states, router_w, expert_weights):
        import jax, jax.numpy as jnp
        import numpy as np
        K_TOP = 2
        B, S, H = hidden_states.shape
        x = hidden_states.reshape(-1, H)
        logits = x @ router_w.T
        probs = jax.nn.softmax(logits, axis=-1)
        topk_vals, topk_idx = jax.lax.top_k(probs, K_TOP)
        topk_w = topk_vals / (topk_vals.sum(-1, keepdims=True) + 1e-06)
        expert_out = jnp.einsum('nh,eho->eno', x, expert_weights)
        combined = jnp.take_along_axis(expert_out.transpose(1, 0, 2), topk_idx[:, :, None], axis=1)
        combined = combined.transpose(1, 0, 2)
        remap_bias = jnp.take_along_axis(probs, topk_idx, axis=1).T[:, :, None]
        weights = topk_w.T[:, :, None]
        out = ((combined + remap_bias) * weights).sum(axis=0)
        return out.reshape(B, S, H)

    def _L1_cond_ref(x, w, W_base, b_base, As, Bs):
        import jax, jax.numpy as jnp
        import numpy as np
        R = 16
        ALPHA = 32.0
        SCALING = ALPHA / R
        out = jnp.einsum('btc,oc->bto', x, W_base) + b_base
        h = jnp.einsum('btc,erc->bter', x, As)
        lora = jnp.einsum('bter,eor,be->bto', h, Bs, w)
        return out + lora * SCALING

    def _L1_ffn_ref(hidden_states, gate_w, exp_gate, exp_up, exp_down, sh_gate, sh_up, sh_down):
        import jax, jax.numpy as jnp
        import numpy as np
        B, L, D = (4, 512, 256)
        E, K, S = (8, 2, 2)
        F = 352
        SCALE = 1.0
        INIT = 0.02

        def _swiglu(x, wg, wu, wd):
            return jax.nn.silu(x @ wg) * (x @ wu) @ wd
        Bx, Lx, Dx = hidden_states.shape
        x = hidden_states.reshape(-1, Dx)
        T = x.shape[0]
        shared = jnp.zeros_like(x)
        for i in range(sh_gate.shape[0]):
            shared = shared + _swiglu(x, sh_gate[i], sh_up[i], sh_down[i])
        logits = x @ gate_w
        probs = jax.nn.softmax(logits.astype(jnp.float32), axis=-1)
        w, sel = jax.lax.top_k(probs, K)
        w = w / jnp.sum(w, axis=-1, keepdims=True)
        w = w.astype(hidden_states.dtype)
        Wte = jnp.zeros((T, exp_gate.shape[0]), hidden_states.dtype)
        Wte = Wte.at[jnp.arange(T)[:, None], sel].add(w)
        routed = jnp.zeros_like(x)
        for e in range(exp_gate.shape[0]):
            routed = routed + Wte[:, e:e + 1] * _swiglu(x, exp_gate[e], exp_up[e], exp_down[e])
        out = shared + SCALE * routed
        return out.reshape(Bx, Lx, Dx)
    x = x + _L0_ffn_ref(_L0_cond_ref(x, cond_8, L0_cond_weight, L0_cond_mask, L0_cond_bias), L0_ffn_router_w, L0_ffn_expert_weights)
    x = x + _L1_ffn_ref(_L1_cond_ref(x, cond_8, L1_cond_W_base, L1_cond_b_base, L1_cond_As, L1_cond_Bs), L1_ffn_gate_w, L1_ffn_exp_gate, L1_ffn_exp_up, L1_ffn_exp_down, L1_ffn_sh_gate, L1_ffn_sh_up, L1_ffn_sh_down)
    return x

_drawn_inputs = setup_inputs


def setup_inputs(seed=0):
    import zlib

    import numpy as np

    out = dict(_drawn_inputs(seed))
    spreads = {}
    factors = {}
    for name, (base, spread) in spreads.items():
        noise = np.random.default_rng([zlib.crc32(name.encode()), seed]).standard_normal(out[name].shape)
        drawn = base * np.exp(spread * noise) if base else spread * noise
        out[name] = jnp.asarray(drawn.astype(out[name].dtype))
    for name, factor in factors.items():
        out[name] = (out[name] * factor).astype(out[name].dtype)
    return out
```

```python
from contextlib import ExitStack

import concourse.bass as bass
from concourse import mybir

ALU = mybir.AluOpType
ACT = mybir.ActivationFunctionType
AX = mybir.AxisListType
F32 = mybir.dt.float32
F16 = mybir.dt.float16
I32 = mybir.dt.int32

P = 128
HI, LO = 0, 1
PASSES = ((HI, HI), (LO, HI), (HI, LO))

SX = 8.0
SWB = 8.0
SH0 = SX * SWB
SW = 64.0
SWC = 32.0
SH1 = SX * SWC
SA = 512.0
LORA_SCALE = 2.0
EPS_TOPK = 1e-6
FAR = 1e30


def build_program(nc, cond_row, cond_er, xT, x, wc, mask, bias0, router, w0, wbase, bias1, lora_a, lora_b,
                  gate, w1, out):
    _, KT, N = xT.shape
    D = KT * P
    B = cond_er.shape[1]
    G = wc.shape[1]
    E = gate.shape[2]
    S = N // B
    NT = N // P
    TPB = S // P
    PAIRS = E // 2
    WE = w1.shape[2]
    NEXP = w1.shape[1]
    FT = 3
    F = (WE - FT * D) // (2 * KT)
    FS = [min(P, F - P * f) for f in range(FT)]
    SHARED = NEXP - E
    FLAT = NEXP * WE
    NP = NT
    PIECE = FLAT // NP
    w1_flat = w1.rearrange("p e w -> p (e w)")

    with ExitStack() as ctx:
        early = ExitStack()

        def sb(name, shape, dt, where=ctx):
            return where.enter_context(nc.sbuf_tensor(name, shape, dt))

        def sem(name):
            return ctx.enter_context(nc.semaphore(name))

        xs = sb("xs", [P, 2, KT, N], F16)
        hs = sb("hs", [P, 2, KT, N], F16)
        x1 = sb("x1", [P, NT, D], F32)
        w0s = sb("w0s", [P, 2, KT, E * D], F16)
        w1s = sb("w1s", [P, 2, FLAT], F16)
        wbs = sb("wbs", [P, B, 2, KT, D], F16)
        wls = sb("wls", [P, B, 2, KT, D], F16)
        rs = sb("rs", [P, 2, 2, KT, E], F16)
        rin = sb("rin", [P, 2, KT, E], F32)
        ycol = sb("ycol", [P, B * G], F32)
        ercol = sb("ercol", [P, B], F32)
        b_in = sb("b_in", [P, 2, KT], F32)
        b_sc = sb("b_sc", [P, 2, KT], F32)
        ident = sb("ident", [P, P], F32)
        rank_e = sb("rank_e", [P, E], F32)
        lbw = sb("lbw", [P, B, D], F32)
        lg = sb("lg", [P, NT, E], F32)
        t1 = sb("t1", [P, NT, E], F32)
        oh1 = sb("oh1", [P, NT, E], F32)
        oh2 = sb("oh2", [P, NT, E], F32)
        coef = sb("coef", [P, NT, E], F32)
        st = sb("st", [P, 12, NT], F32)
        M1, K1, M2, K2, SUM, P1, P2, DEN, W1, W2, BIAS, TMP = (st[:, i, :] for i in range(12))

        wc_in = x1[:, :, :].rearrange("p a b -> p (a b)").rearrange("p (g w) -> p g w", g=G)
        x_in = sb("x_in", [P, 2, KT, S], F32, early)
        mask_in = sb("mask_in", [P, KT * D], F32, early)
        wacc = sb("wacc", [P, 2, KT * D], F32, early)
        w0_in = sb("w0_in", [P, 2, 1024], F32, early)
        la = sb("la", [P, D], F32, early)
        lb = sb("lb", [P, D], F32, early)
        wb_in = sb("wb_in", [P, KT * D], F32, early)
        early.close()
        piece = sb("piece", [P, 2, PIECE], F32)
        sil = sb("sil", [P, 2, S], F32)
        prod = sb("prod", [P, 2, S], F32)
        acts = sb("acts", [P, 2, FT, 2, S], F16)

        bank = [ctx.enter_context(nc.psum_tensor(f"bank{i}", [P, 512], F32)) for i in range(8)]

        names = ("s_small s_wc s_mask s_w0c s_xm s_bsc s_lbw s_lora s_wacc s_wbhi s_wblo s_xhi s_xlo "
                 "s_h s_hhi s_hlo s_w0hi s_w0lo s_wlf s_wlhi s_wllo s_log s_dve s_exp s_exq s_r0 s_ffn s_comb s_bias "
                 "s_tr s_trhi s_trlo s_pchi s_pclo s_gu s_sil s_prod s_ahi s_alo s_dn s_acc s_id s_rank s_rsp s_out").split()
        sm = {n: sem(n) for n in names}
        s_xin = [sem(f"s_xin{c}") for c in range(B)]
        s_w0in = [sem(f"s_w0in{c}") for c in range(4)]
        s_piece = [sem(f"s_piece{c}") for c in range(NP)]
        block = ctx.enter_context(nc.Block())
        UN = B * NEXP

        def w_gu(hl, e, k, g, f):
            o = e * WE + k * 2 * F + g * F + f * P
            return w1s[:, hl, o:o + FS[f]]

        def w_dn(hl, e, f):
            o = e * WE + KT * 2 * F + f * D
            return w1s[0:FS[f], hl, o:o + D]

        @block.sync
        def _(sp):
            sp.dma_start(ycol[:], cond_row.partition_broadcast(P).rearrange("p a n -> p (a n)")).then_inc(sm["s_small"], 16)
            sp.dma_start(wc_in[:, 0:4, :], wc[:, 0:4, :]).then_inc(sm["s_wc"], 16)
            sp.dma_start(wc_in[:, 4:8, :], wc[:, 4:8, :]).then_inc(sm["s_wc"], 16)
            sp.dma_start(mask_in[:], mask).then_inc(sm["s_mask"], 16)
            for c in range(B):
                if c >= 2:
                    sp.wait_ge(sm["s_xlo"], c - 1)
                sp.dma_start(x_in[:, c % 2], xT[:, :, c * S:(c + 1) * S]).then_inc(s_xin[c], 16)
            for i in range(4):
                if i >= 2:
                    sp.wait_ge(sm["s_w0lo"], i - 1)
                sp.dma_start(w0_in[:, i % 2], w0[:, i * 1024:(i + 1) * 1024]).then_inc(s_w0in[i], 16)
            sp.wait_ge(sm["s_wacc"], B)
            sp.dma_start(x1[:], x).then_inc(sm["s_xm"], 16)
            for i in range(NP):
                if i == 0:
                    sp.wait_ge(sm["s_xlo"], B)
                    sp.wait_ge(sm["s_w0lo"], 4)
                    sp.wait_ge(sm["s_wblo"], B)
                if i >= 2:
                    sp.wait_ge(sm["s_pclo"], i - 1)
                sp.dma_start(piece[:, i % 2], w1_flat[:, i * PIECE:(i + 1) * PIECE]).then_inc(s_piece[i], 16)
            for b in range(B):
                sp.wait_ge(sm["s_acc"], (UN - B + b + 1) * TPB)
                sp.dma_start(out[:, b * TPB:(b + 1) * TPB], x1[:, b * TPB:(b + 1) * TPB]).then_inc(sm["s_out"], 16)
            sp.wait_ge(sm["s_out"], 16 * B)

        @block.gpsimd
        def _(pool):
            nc.gpsimd.memset(ident[:], 0.0).then_inc(sm["s_id"], 1)
            pool.wait_ge(sm["s_id"], 1)
            nc.gpsimd.affine_select(out=ident[:], in_=ident[:], compare_op=ALU.not_equal, fill=1.0, base=0,
                                    pattern=[[-1, P]], channel_multiplier=1).then_inc(sm["s_id"], 1)
            nc.gpsimd.iota(rank_e[:], [[-1, E]], base=E, channel_multiplier=0,
                           allow_small_or_imprecise_dtypes=True).then_inc(sm["s_rank"], 1)

        @block.scalar
        def _(act):
            act.dma_start(rin[:, 0], router).then_inc(sm["s_small"], 16)
            act.dma_start(rin[:, 1], gate).then_inc(sm["s_small"], 16)
            act.dma_start(b_in[:, 0], bias0).then_inc(sm["s_small"], 16)
            act.dma_start(b_in[:, 1], bias1).then_inc(sm["s_small"], 16)
            act.dma_start(ercol[:], cond_er).then_inc(sm["s_small"], 16)
            act.dma_start(la[:], lora_a).then_inc(sm["s_small"], 16)
            act.dma_start(lb[:], lora_b).then_inc(sm["s_small"], 16)
            act.dma_start(wb_in[:], wbase).then_inc(sm["s_small"], 16)
            def h_hi(layer, c):
                for o in range(KT):
                    i = layer * B * KT + c * KT + o
                    act.wait_ge(sm["s_h"], i + 1)
                    nc.scalar.activation(hs[:, HI, o, c * S:(c + 1) * S], bank[4 + i % 2][:], ACT.Identity,
                                         bias=b_sc[:, layer, o:o + 1]).then_inc(sm["s_hhi"], 1)

            for c in range(B):
                act.wait_ge(s_xin[c], 16)
                nc.scalar.activation(xs[:, HI, :, c * S:(c + 1) * S], x_in[:, c % 2], ACT.Copy,
                                     scale=SX).then_inc(sm["s_xhi"], 1)
                if c == 0:
                    act.wait_ge(sm["s_small"], 16 * 9)
                    nc.scalar.activation(rs[:, :, HI], rin[:], ACT.Copy, scale=SW).then_inc(sm["s_rsp"], 1)
                act.wait_ge(sm["s_wacc"], c + 1)
                nc.scalar.activation(wbs[:, c, HI].rearrange("p a b -> p (a b)"), wacc[:, c % 2],
                                     ACT.Copy).then_inc(sm["s_wbhi"], 1)
                act.wait_ge(sm["s_bsc"], 1)
                h_hi(0, c)
            for i in range(4):
                act.wait_ge(s_w0in[i], 16)
                nc.scalar.activation(w0s[:, HI].rearrange("p a b -> p (a b)")[:, i * 1024:(i + 1) * 1024],
                                     w0_in[:, i % 2], ACT.Copy, scale=SW).then_inc(sm["s_w0hi"], 1)
            for b in range(B):
                act.wait_ge(sm["s_wlf"], b + 1)
                nc.scalar.activation(wls[:, b, HI].rearrange("p a b -> p (a b)"), lbw[:, 2 * (b % 2):2 * (b % 2) + 2, :].rearrange("p a b -> p (a b)"),
                                     ACT.Copy).then_inc(sm["s_wlhi"], 1)

            def exps(layer):
                scale = 1.0 / (SH0 * SW) if layer == 0 else 1.0 / (SH1 * SW)
                act.wait_ge(sm["s_exq"], layer + 1)
                nc.scalar.activation(t1[:], t1[:], ACT.Exp, scale=scale).then_inc(sm["s_exp"], 1)
                nc.scalar.activation(P2, TMP, ACT.Exp, scale=scale).then_inc(sm["s_exp"], 1)

            exps(0)
            act.wait_ge(sm["s_xm"], 16)
            act.wait_ge(sm["s_r0"], 1)
            for t in range(NT):
                nc.scalar.activation(x1[:, t], x1[:, t], ACT.Identity, bias=BIAS[:, t:t + 1]).then_inc(sm["s_bias"], 1)
            for t in range(NT):
                act.wait_ge(s_piece[t], 16)
                nc.scalar.activation(w1s[:, HI, t * PIECE:(t + 1) * PIECE], piece[:, t % 2], ACT.Copy,
                                     scale=SW).then_inc(sm["s_pchi"], 1)
                act.wait_ge(sm["s_tr"], t + 1)
                nc.scalar.activation(xs[:, HI, :, t * P:(t + 1) * P],
                                     bank[6 + t % 2][:, 0:D].rearrange("p (k n) -> p k n", k=KT),
                                     ACT.Copy, scale=SX).then_inc(sm["s_trhi"], 1)
            for c in range(B):
                h_hi(1, c)
            exps(1)
            for u in range(UN):
                for f in range(FT):
                    i = u * FT + f
                    M = FS[f]
                    act.wait_ge(sm["s_gu"], i + 1)
                    if i >= 2:
                        act.wait_ge(sm["s_prod"], i - 1)
                    nc.scalar.activation(sil[0:M, i % 2], bank[2 * (i % 2)][0:M], ACT.Silu,
                                         scale=1.0 / (SH1 * SW)).then_inc(sm["s_sil"], 1)
                    act.wait_ge(sm["s_prod"], i + 1)
                    if f == 0 and u >= 2:
                        act.wait_ge(sm["s_dn"], (u - 1) * TPB)
                    nc.scalar.activation(acts[0:M, u % 2, f, HI], prod[0:M, i % 2], ACT.Copy).then_inc(sm["s_ahi"], 1)

        @block.vector
        def _(dve):
            chain = [0]

            def link(ins):
                chain[0] += 1
                ins.then_inc(sm["s_dve"], 1)
                dve.wait_ge(sm["s_dve"], chain[0])

            def h_lo(layer, c):
                for o in range(KT):
                    i = layer * B * KT + c * KT + o
                    dve.wait_ge(sm["s_hhi"], i + 1)
                    nc.vector.scalar_tensor_tensor(hs[:, LO, o, c * S:(c + 1) * S], bank[4 + i % 2][:],
                                                   b_sc[:, layer, o:o + 1], hs[:, HI, o, c * S:(c + 1) * S],
                                                   ALU.add, ALU.subtract).then_inc(sm["s_hlo"], 1)

            def x_lo(c):
                dve.wait_ge(sm["s_xhi"], c + 1)
                nc.vector.scalar_tensor_tensor(xs[:, LO, :, c * S:(c + 1) * S], x_in[:, c % 2], SX,
                                               xs[:, HI, :, c * S:(c + 1) * S],
                                               ALU.mult, ALU.subtract).then_inc(sm["s_xlo"], 1)

            dve.wait_ge(sm["s_small"], 16 * 9)
            link(nc.vector.tensor_scalar(b_sc[:, 0], b_in[:, 0], SH0, None, ALU.mult))
            nc.vector.tensor_scalar(b_sc[:, 1], b_in[:, 1], SH1, None, ALU.mult).then_inc(sm["s_bsc"], 1)
            for b in range(B):
                nc.vector.tensor_scalar(lbw[:, b], lb[:], ercol[:, b:b + 1], LORA_SCALE * SWC, ALU.mult,
                                        ALU.mult).then_inc(sm["s_lbw"], 1)
            dve.wait_ge(sm["s_wc"], 32)
            dve.wait_ge(sm["s_mask"], 16)
            for b in range(B):
                if b >= 2:
                    dve.wait_ge(sm["s_wblo"], b - 1)
                w = wacc[:, b % 2]
                link(nc.vector.tensor_scalar(w, wc_in[:, 0], ycol[:, b * G:b * G + 1], None, ALU.mult))
                for g in range(1, G):
                    link(nc.vector.scalar_tensor_tensor(w, wc_in[:, g], ycol[:, b * G + g:b * G + g + 1], w,
                                                        ALU.mult, ALU.add))
                nc.vector.scalar_tensor_tensor(w, w, SWB, mask_in[:], ALU.mult, ALU.mult).then_inc(sm["s_wacc"], 1)
                x_lo(b)
                dve.wait_ge(sm["s_wbhi"], b + 1)
                nc.vector.tensor_tensor(wbs[:, b, LO].rearrange("p a b -> p (a b)"), w,
                                        wbs[:, b, HI].rearrange("p a b -> p (a b)"),
                                        ALU.subtract).then_inc(sm["s_wblo"], 1)
                if b == 0:
                    dve.wait_ge(sm["s_rsp"], 1)
                    nc.vector.scalar_tensor_tensor(rs[:, :, LO].rearrange("p a k e -> p a (k e)"),
                                                   rin[:].rearrange("p a k e -> p a (k e)"), SW,
                                                   rs[:, :, HI].rearrange("p a k e -> p a (k e)"),
                                                   ALU.mult, ALU.subtract).then_inc(sm["s_rsp"], 1)
                if b >= 1:
                    h_lo(0, b - 1)
            h_lo(0, B - 1)
            for i in range(4):
                dve.wait_ge(sm["s_w0hi"], i + 1)
                nc.vector.scalar_tensor_tensor(w0s[:, LO].rearrange("p a b -> p (a b)")[:, i * 1024:(i + 1) * 1024],
                                               w0_in[:, i % 2], SW,
                                               w0s[:, HI].rearrange("p a b -> p (a b)")[:, i * 1024:(i + 1) * 1024],
                                               ALU.mult, ALU.subtract).then_inc(sm["s_w0lo"], 1)
            dve.wait_ge(sm["s_lora"], B)
            for b in range(B):
                wl = lbw[:, 2 * (b % 2):2 * (b % 2) + 2, :].rearrange("p a b -> p (a b)")
                if b >= 2:
                    dve.wait_ge(sm["s_wllo"], b - 1)
                nc.vector.scalar_tensor_tensor(wl, wb_in[:], SWC, bank[b][:], ALU.mult,
                                               ALU.add).then_inc(sm["s_wlf"], 1)
                dve.wait_ge(sm["s_wlhi"], b + 1)
                nc.vector.tensor_tensor(wls[:, b, LO].rearrange("p a b -> p (a b)"), wl,
                                        wls[:, b, HI].rearrange("p a b -> p (a b)"),
                                        ALU.subtract).then_inc(sm["s_wllo"], 1)

            def each(a):
                return a.unsqueeze(2).to_broadcast([P, NT, E])

            def top(src, best, key, onehot):
                link(nc.vector.tensor_reduce(best, src, AX.X, ALU.max))
                link(nc.vector.tensor_tensor(t1[:], src, each(best), ALU.is_equal))
                link(nc.vector.tensor_tensor(t1[:], t1[:], rank_e[:].unsqueeze(1).to_broadcast([P, NT, E]), ALU.mult))
                link(nc.vector.tensor_reduce(key, t1[:], AX.X, ALU.max))
                link(nc.vector.tensor_tensor(onehot[:], t1[:], each(key), ALU.is_equal))

            def route(layer):
                dve.wait_ge(sm["s_log"], layer + 1)
                dve.wait_ge(sm["s_rank"], 1)
                link(nc.vector.tensor_copy(lg[:].rearrange("p t e -> p (t e)"), bank[6][:, 0:NT * E]))
                top(lg[:], M1, K1, oh1)
                link(nc.vector.scalar_tensor_tensor(coef[:], oh1[:], -FAR, lg[:], ALU.mult, ALU.add))
                top(coef[:], M2, K2, oh2)
                link(nc.vector.tensor_tensor(TMP, M2, M1, ALU.subtract))
                nc.vector.tensor_tensor(t1[:], lg[:], each(M1), ALU.subtract).then_inc(sm["s_exq"], 1)
                dve.wait_ge(sm["s_exp"], 2 * layer + 2)
                link(nc.vector.tensor_reduce(SUM, t1[:], AX.X, ALU.add))
                link(nc.vector.reciprocal(P1, SUM))
                link(nc.vector.tensor_tensor(P2, P2, P1, ALU.mult))
                link(nc.vector.tensor_tensor(DEN, P1, P2, ALU.add))
                if layer == 0:
                    link(nc.vector.tensor_scalar(DEN, DEN, EPS_TOPK, None, ALU.add))
                link(nc.vector.reciprocal(DEN, DEN))
                link(nc.vector.tensor_tensor(W1, P1, DEN, ALU.mult))
                link(nc.vector.tensor_tensor(W2, P2, DEN, ALU.mult))
                if layer == 0:
                    link(nc.vector.tensor_tensor(BIAS, P1, W1, ALU.mult))
                    link(nc.vector.tensor_tensor(TMP, P2, W2, ALU.mult))
                    nc.vector.tensor_tensor(BIAS, BIAS, TMP, ALU.add).then_inc(sm["s_r0"], 1)
                scale = 1.0 / (SH0 * SW) if layer == 0 else 1.0 / (SA * SW)
                link(nc.vector.tensor_scalar(W1, W1, scale, None, ALU.mult))
                link(nc.vector.tensor_scalar(W2, W2, scale, None, ALU.mult))
                link(nc.vector.tensor_tensor(t1[:], oh1[:], each(W1), ALU.mult))
                link(nc.vector.tensor_tensor(coef[:], oh2[:], each(W2), ALU.mult))
                link(nc.vector.tensor_tensor(coef[:], coef[:], t1[:], ALU.add))

            route(0)

            def tr_lo(t):
                dve.wait_ge(sm["s_trhi"], t + 1)
                nc.vector.scalar_tensor_tensor(xs[:, LO, :, t * P:(t + 1) * P],
                                               bank[6 + t % 2][:, 0:D].rearrange("p (k n) -> p k n", k=KT),
                                               SX, xs[:, HI, :, t * P:(t + 1) * P],
                                               ALU.mult, ALU.subtract).then_inc(sm["s_trlo"], 1)

            for t in range(NT):
                dve.wait_ge(sm["s_bias"], t + 1)
                for j in range(PAIRS):
                    dve.wait_ge(sm["s_ffn"], t * PAIRS + j + 1)
                    for h in range(2):
                        e = 2 * j + h
                        ins = nc.vector.scalar_tensor_tensor(x1[:, t], bank[j][:, h * D:(h + 1) * D],
                                                             coef[:, t, e:e + 1], x1[:, t], ALU.mult, ALU.add)
                        ins.then_inc(sm["s_comb"], 1)
                        dve.wait_ge(sm["s_comb"], t * E + e + 1)
                dve.wait_ge(sm["s_pchi"], t + 1)
                nc.vector.scalar_tensor_tensor(w1s[:, LO, t * PIECE:(t + 1) * PIECE], piece[:, t % 2], SW,
                                               w1s[:, HI, t * PIECE:(t + 1) * PIECE],
                                               ALU.mult, ALU.subtract).then_inc(sm["s_pclo"], 1)
                if t >= 1:
                    tr_lo(t - 1)
            tr_lo(NT - 1)
            for c in range(B):
                h_lo(1, c)
            route(1)

            def accumulate(u):
                b, e = u % B, u // B
                for q in range(TPB):
                    i = u * TPB + q
                    t = b * TPB + q
                    dve.wait_ge(sm["s_dn"], i + 1)
                    if u >= B:
                        dve.wait_ge(sm["s_acc"], (u - B) * TPB + q + 1)
                    w = 1.0 / (SA * SW) if e < SHARED else coef[:, t, e - SHARED:e - SHARED + 1]
                    nc.vector.scalar_tensor_tensor(x1[:, t], bank[4 + i % 2][:, 0:D], w, x1[:, t], ALU.mult,
                                                   ALU.add).then_inc(sm["s_acc"], 1)

            for u in range(UN):
                for f in range(FT):
                    i = u * FT + f
                    M = FS[f]
                    dve.wait_ge(sm["s_sil"], i + 1)
                    if i >= 2:
                        dve.wait_ge(sm["s_alo"], i - 1)
                        dve.wait_ge(sm["s_ahi"], i - 1)
                    nc.vector.scalar_tensor_tensor(prod[0:M, i % 2], bank[2 * (i % 2) + 1][0:M],
                                                   SA / (SH1 * SW), sil[0:M, i % 2], ALU.mult,
                                                   ALU.mult).then_inc(sm["s_prod"], 1)
                    dve.wait_ge(sm["s_ahi"], i + 1)
                    nc.vector.tensor_tensor(acts[0:M, u % 2, f, LO], prod[0:M, i % 2], acts[0:M, u % 2, f, HI],
                                            ALU.subtract).then_inc(sm["s_alo"], 1)
                    if f == 1 and u >= 1:
                        accumulate(u - 1)
            accumulate(UN - 1)

        @block.tensor
        def _(pe):
            def group(out_ap, terms, s=None, n=1):
                for i, (l, r) in enumerate(terms):
                    mm = nc.tensor.matmul(out_ap, l, r, start=(i == 0), stop=(i == len(terms) - 1))
                if s is not None:
                    mm.then_inc(sm[s], n)
                return mm

            pe.wait_ge(sm["s_small"], 16 * 9)
            for b in range(B):
                pe.wait_ge(sm["s_lbw"], b + 1)
                for k in range(KT):
                    mm = nc.tensor.matmul(bank[b][:, k * D:(k + 1) * D], la[:, k * P:(k + 1) * P], lbw[:, b],
                                          start=True, stop=True)
                mm.then_inc(sm["s_lora"], 1)

            def project(layer, c):
                w = wbs if layer == 0 else wls
                for o in range(KT):
                    i = layer * B * KT + c * KT + o
                    if i >= 2:
                        pe.wait_ge(sm["s_hlo"], i - 1)
                    group(bank[4 + i % 2][:], [(w[:, c, a, k, o * P:(o + 1) * P], xs[:, b, k, c * S:(c + 1) * S])
                                               for k in range(KT) for a, b in PASSES], "s_h")

            def logits(layer):
                for t in range(NT):
                    mm = group(bank[6][:, t * E:(t + 1) * E],
                               [(hs[:, a, k, t * P:(t + 1) * P], rs[:, layer, b, k, :])
                                for k in range(KT) for a, b in PASSES])
                mm.then_inc(sm["s_log"], 1)

            for c in range(B):
                pe.wait_ge(sm["s_xlo"], c + 1)
                pe.wait_ge(sm["s_wblo"], c + 1)
                project(0, c)
            pe.wait_ge(sm["s_rsp"], 2)
            pe.wait_ge(sm["s_hlo"], B * KT)
            logits(0)
            pe.wait_ge(sm["s_w0lo"], 4)
            pe.wait_ge(sm["s_wlf"], B)
            pe.wait_ge(sm["s_id"], 2)

            def transposes(t):
                pe.wait_ge(sm["s_comb"], (t + 1) * E)
                if t >= 2:
                    pe.wait_ge(sm["s_trlo"], t - 1)
                for k in range(KT):
                    mm = nc.tensor.transpose(bank[6 + t % 2][:, k * P:(k + 1) * P],
                                             x1[:, t, k * P:(k + 1) * P], ident[:])
                mm.then_inc(sm["s_tr"], 1)

            for t in range(NT):
                for j in range(PAIRS):
                    if t >= 1:
                        pe.wait_ge(sm["s_comb"], (t - 1) * E + 2 * j + 2)
                    group(bank[j][:], [(hs[:, a, k, t * P:(t + 1) * P], w0s[:, b, k, j * 2 * D:(j + 1) * 2 * D])
                                       for k in range(KT) for a, b in PASSES], "s_ffn")
                if t >= 1:
                    transposes(t - 1)
            transposes(NT - 1)
            pe.wait_ge(sm["s_trlo"], NT)
            pe.wait_ge(sm["s_wllo"], B)
            for c in range(B):
                project(1, c)
            pe.wait_ge(sm["s_hlo"], 2 * B * KT)
            logits(1)
            pe.wait_ge(sm["s_pclo"], NP)

            def down(u):
                e = u // B
                pe.wait_ge(sm["s_alo"], (u + 1) * FT)
                for q in range(TPB):
                    i = u * TPB + q
                    if i >= 2:
                        pe.wait_ge(sm["s_acc"], i - 1)
                    group(bank[4 + i % 2][:, 0:D], [(acts[0:FS[f], u % 2, f, a, q * P:(q + 1) * P], w_dn(b, e, f))
                                                    for f in range(FT) for a, b in PASSES], "s_dn")

            for u in range(UN):
                c, e = u % B, u // B
                for f in range(FT):
                    i = u * FT + f
                    if i >= 2:
                        pe.wait_ge(sm["s_prod"], i - 1)
                    for g in range(2):
                        mm = group(bank[2 * (i % 2) + g][0:FS[f]],
                                   [(w_gu(a, e, k, g, f), hs[:, b, k, c * S:(c + 1) * S])
                                    for k in range(KT) for a, b in PASSES])
                    mm.then_inc(sm["s_gu"], 1)
                    if f == 1 and u >= 1:
                        down(u - 1)
            down(UN - 1)


def kernel(x, cond_8, L0_cond_weight, L0_cond_mask, L0_cond_bias, L0_ffn_router_w, L0_ffn_expert_weights,
           L1_cond_W_base, L1_cond_b_base, L1_cond_As, L1_cond_Bs, L1_ffn_gate_w, L1_ffn_exp_gate,
           L1_ffn_exp_up, L1_ffn_exp_down, L1_ffn_sh_gate, L1_ffn_sh_up, L1_ffn_sh_down):
    import numpy as np
    import concourse.bacc as bacc
    from concourse.bass_utils import run_bass_kernel_spmd

    Bb, S, D = x.shape
    N, KT = Bb * S, D // P
    E, R, _ = L1_cond_As.shape
    F = L1_ffn_exp_gate.shape[2]

    def by_k(a):
        return np.ascontiguousarray(a.reshape(KT, P, -1).transpose(1, 0, 2))

    def swiglu_rows(wg, wu, wd):
        n = wg.shape[0]
        gu = np.concatenate([wg, wu], axis=2).reshape(n, KT, P, 2 * F).transpose(2, 0, 1, 3).reshape(P, n, -1)
        ft = -(-F // P)
        dn = np.zeros((n, ft * P, D), wd.dtype)
        dn[:, :F] = wd
        dn = dn.reshape(n, ft, P, D).transpose(2, 0, 1, 3).reshape(P, n, -1)
        return np.concatenate([gu, dn], axis=2)

    x = np.asarray(x)
    tok = x.reshape(N, D)
    c = np.asarray
    ins = {
        "cond_row": c(cond_8).reshape(1, -1),
        "cond_er": np.ascontiguousarray(np.repeat(c(cond_8).T, R, axis=0)),
        "xT": by_k(tok.T),
        "x": np.ascontiguousarray(tok.reshape(N // P, P, D).transpose(1, 0, 2)),
        "wc": np.ascontiguousarray(c(L0_cond_weight).reshape(E, D, KT, P).transpose(3, 0, 2, 1).reshape(P, E, KT * D)),
        "mask": by_k(c(L0_cond_mask).T).reshape(P, KT * D),
        "bias0": np.ascontiguousarray(c(L0_cond_bias).reshape(KT, P).T),
        "router": by_k(c(L0_ffn_router_w).T),
        "w0": by_k(c(L0_ffn_expert_weights).transpose(1, 0, 2).reshape(D, E * D)).reshape(P, KT * E * D),
        "wbase": by_k(c(L1_cond_W_base).T).reshape(P, KT * D),
        "bias1": np.ascontiguousarray(c(L1_cond_b_base).reshape(KT, P).T),
        "lora_a": c(L1_cond_As).reshape(E * R, D),
        "lora_b": np.ascontiguousarray(c(L1_cond_Bs).transpose(0, 2, 1).reshape(E * R, D)),
        "gate": by_k(c(L1_ffn_gate_w)),
        "w1": np.ascontiguousarray(np.concatenate(
            [swiglu_rows(c(L1_ffn_sh_gate), c(L1_ffn_sh_up), c(L1_ffn_sh_down)),
             swiglu_rows(c(L1_ffn_exp_gate), c(L1_ffn_exp_up), c(L1_ffn_exp_down))], axis=1)),
    }
    nc = bacc.Bacc("TRN2", target_bir_lowering=False, num_devices=1)
    aps = {n: nc.dram_tensor(n, a.shape, mybir.dt.from_np(a.dtype), kind="ExternalInput").ap()
           for n, a in ins.items()}
    out = nc.dram_tensor("out", (P, N // P, D), F32, kind="ExternalOutput").ap()
    build_program(nc, out=out, **aps)
    r = run_bass_kernel_spmd(nc, [ins], core_ids=[0])
    return r.results[0]["out"].reshape(P, N // P, D).transpose(1, 0, 2).reshape(Bb, S, D)
```

```python
from contextlib import ExitStack

import concourse.bass as bass
from concourse import mybir

ALU = mybir.AluOpType
ACT = mybir.ActivationFunctionType
AX = mybir.AxisListType
F32 = mybir.dt.float32
F16 = mybir.dt.float16
I32 = mybir.dt.int32

P = 128
HI, LO = 0, 1
PASSES = ((HI, HI), (LO, HI), (HI, LO))

SX = 8.0
SWB = 8.0
SH0 = SX * SWB
SW = 64.0
SWC = 32.0
SH1 = SX * SWC
SA = 512.0
LORA_SCALE = 2.0
EPS_TOPK = 1e-6
FAR = 1e30


def build_program(nc, cond_row, cond_er, xT, x, wc, mask, bias0, router, w0, wbase, bias1, lora_a, lora_b,
                  gate, w1, out):
    _, KT, N = xT.shape
    D = KT * P
    B = cond_er.shape[1]
    G = wc.shape[1]
    E = gate.shape[2]
    S = N // B
    NT = N // P
    TPB = S // P
    PAIRS = E // 2
    PW = 2 * D
    NEXP, WE = w1.shape[1:]
    FT = 3
    F = (WE - FT * D) // (2 * KT)
    FS = [min(P, F - P * f) for f in range(FT)]
    SHARED = NEXP - E
    FLAT = NEXP * WE
    NP = NT
    PIECE = FLAT // NP
    K_TOP = 2
    TILES = (N * K_TOP + E * (P - 1)) // P
    PAD = E // 2
    LOOPS = (TILES - 5) // 2
    UN = SHARED * B
    w1_flat = w1.rearrange("p e w -> p (e w)")
    slot_rows = nc.dram_tensor("slot_rows", (TILES * P, 2 * D), F16).ap()
    slot_out = nc.dram_tensor("slot_out", (TILES * P, D), F32).ap()

    with ExitStack() as ctx:
        def sb(name, shape, dt, where=ctx):
            return where.enter_context(nc.sbuf_tensor(name, shape, dt))

        def sem(name):
            return ctx.enter_context(nc.semaphore(name))

        def flat(ap):
            return ap.rearrange("p a b -> p (a b)")

        xs = sb("xs", [P, NT, 2, KT, P], F16)
        hs = sb("hs", [P, 2, KT, N], F16)
        x1 = sb("x1", [P, NT, D], F32)
        w1s = sb("w1s", [P, 2, FLAT], F16)
        wls = sb("wls", [P, B, 2, KT, D], F16)
        rs = sb("rs", [P, 2, 2, KT, E], F16)
        rin = sb("rin", [P, 2, KT, E], F32)
        ycol = sb("ycol", [P, B * G], F32)
        ercol = sb("ercol", [P, B], F32)
        b_in = sb("b_in", [P, 2, KT], F32)
        b_sc = sb("b_sc", [P, 2, KT], F32)
        ident = sb("ident", [P, P], F32)
        ident16 = sb("ident16", [P, P], F16)
        before = sb("before", [P, P], F16)
        ones16 = sb("ones16", [P, P], F16)
        zrow = sb("zrow", [P, 2 * D], F16)
        rank_e = sb("rank_e", [P, E], F32)
        tile_no = sb("tile_no", [1, TILES, E], F32)
        t1 = sb("t1", [P, NT, E], F32)
        t2 = sb("t2", [P, NT, E], F32)
        ex = sb("ex", [P, NT, E], F32)
        oh1 = sb("oh1", [P, NT, E], F32)
        oh2 = sb("oh2", [P, NT, E], F32)
        coef = sb("coef", [P, NT, E], F32)
        sel16 = sb("sel16", [P, 2 * NT, E], F16)
        st = sb("st", [P, 9, NT], F32)
        M1, K1, M2, SUM, S2, REC, BIAS, W1, W2 = (st[:, i, :] for i in range(9))
        cnt = sb("cnt", [P, E], I32)
        scan = sb("scan", [P, 2, PAD + E], F32)
        base = sb("base", [P, E], F32)
        idx = sb("idx", [P, 2, NT], I32)
        tef = sb("tef", [1, TILES], F32)
        te = sb("te", [1, TILES], I32)
        te4 = sb("te4", [1, LOOPS, 4], I32)
        exp_warm = sb("exp_warm", [1, 1], F32)

        l0 = ExitStack()
        w0s = sb("w0s", [P, 2, KT, E * D], F16, l0)
        first = ExitStack()
        wbs = sb("wbs", [P, B, 2, KT, D], F16, first)
        x_in = sb("x_in", [P, 2, KT, S], F32, first)
        mask_in = sb("mask_in", [P, KT * D], F32, first)
        wacc = sb("wacc", [P, B, KT * D], F32, first)
        first.close()
        second = ExitStack()
        piece = sb("piece", [P, 2, PIECE], F32, second)
        la = sb("la", [P, D], F32, second)
        lb = sb("lb", [P, D], F32, second)
        lbw = sb("lbw", [P, 2, D], F32, second)
        wb_in = sb("wb_in", [P, KT * D], F32, second)
        wl = sb("wl", [P, 2, KT * D], F32, second)
        second.close()
        l0.close()
        sil = sb("sil", [P, 2, S], F32)
        prod = sb("prod", [P, 2, S], F32)
        acts = sb("acts", [P, 2, FT, 2, S], F16)
        rows = sb("rows", [P, 2, 2 * D], F16)
        rT = sb("rT", [P, 2, 2, KT, P], F16)
        ract = sb("ract", [P, 2, 2, F], F16)
        aT = sb("aT", [P, 2, FT, 2, P], F16)
        yb = sb("yb", [P, 2, D], F32)
        yg = sb("yg", [P, 4, K_TOP, D], F32)

        wc_in = x1[:].rearrange("p a b -> p (a b)").rearrange("p (g w) -> p g w", g=G)
        w0_in = [w1s[:, hl, FLAT - 2 * KT * PW:].bitcast(F32).rearrange("p (k w) -> p k w", k=KT) for hl in range(2)]
        diag_at = FLAT - 2 * KT * PW - 2 * 2 * G * P
        diag = w1s[:, HI, diag_at:diag_at + 2 * 2 * G * P].bitcast(F32).rearrange("p (b g m) -> p b g m", b=2, g=G)

        bank = [ctx.enter_context(nc.psum_tensor(f"bank{i}", [P, 512], F32)) for i in range(8)]
        bank16 = [b[:].bitcast(F16) for b in bank]

        names = ("s_small s_mask s_xm s_bsc s_lbw s_lora s_wacc s_wbhi s_wblo s_xhi s_xsc s_xlo s_diag s_wbp "
                 "s_h s_hhi s_hlo s_w0hi s_w0sc s_w0lo s_wlf s_wlhi s_wllo s_log s_dve s_pool s_exp s_exq s_r0 s_ffn "
                 "s_comb s_bias s_tr s_trhi s_trlo s_pchi s_pcsc s_pclo s_gu s_sil s_prod s_ahi s_alo s_dn s_acc "
                 "s_const s_rsp s_out s_lw s_zero s_rt s_rows s_sel s_rank s_idx s_scat s_w12 "
                 "s_ra s_rx s_rg s_ru s_rsil s_rprod s_rhi s_rlo s_rc s_rcx s_rd s_ry s_cmb").split()
        sm = {n: sem(n) for n in names}
        s_wc = [sem(f"s_wc{c}") for c in range(4)]
        s_xin = [sem(f"s_xin{c}") for c in range(B)]
        s_w0in = [sem(f"s_w0in{c}") for c in range(PAIRS)]
        s_piece = [sem(f"s_piece{c}") for c in range(NP)]
        s_row = [sem(f"s_row{c}") for c in range(2)]
        s_yst = [sem(f"s_yst{c}") for c in range(2)]
        s_yg = [sem(f"s_yg{c}") for c in range(4)]
        SMALL = 16 * 6
        block = ctx.enter_context(nc.Block())

        def w_gu(hl, e, k, g, f):
            o = e * WE + k * 2 * F + g * F + f * P
            return w1s[:, hl, o:o + FS[f]]

        def w_dn(hl, e, f):
            o = e * WE + KT * 2 * F + f * D
            return w1s[0:FS[f], hl, o:o + D]

        def chunk(c, hl):
            return xs[:, c * TPB:(c + 1) * TPB, hl].rearrange("p t k n -> p k t n")

        def known(i):
            return not isinstance(i, int) or 0 <= i < TILES

        def again(i):
            return not isinstance(i, int) or i >= 2

        def landed(i, par):
            return i * 8 + (16 - 8 * par)

        def run_tiles(eng, step, ahead):
            for s in range(-2, 3):
                step(s, s % 2)
            pairs = (TILES - 3 - ahead) // 2
            with eng.Fori(0, pairs) as j:
                step(j * 2 + 3, 1)
                step(j * 2 + 4, 0)
            for s in range(3 + 2 * pairs, TILES + 1):
                step(s, s % 2)

        @block.sync
        def _(sp):
            sp.dma_start(ycol[:], cond_row.partition_broadcast(P).rearrange("p a n -> p (a n)")).then_inc(sm["s_small"], 16)
            for i in range(4):
                sp.dma_start(wc_in[:, 2 * i:2 * i + 2, :], wc[:, 2 * i:2 * i + 2, :]).then_inc(s_wc[i], 16)
            sp.dma_start(mask_in[:], mask).then_inc(sm["s_mask"], 16)
            for c in range(B):
                if c >= 2:
                    sp.wait_ge(sm["s_xlo"], c - 1)
                sp.dma_start(x_in[:, c % 2], xT[:, :, c * S:(c + 1) * S]).then_inc(s_xin[c], 16)
                if c >= 2:
                    sp.dma_start(w0_in[c - 2], w0[:, :, (c - 2) * PW:(c - 1) * PW]).then_inc(s_w0in[c - 2], 16)
            sp.wait_ge(sm["s_wacc"], 2)
            sp.wait_ge(sm["s_wbp"], 1)
            sp.dma_start(x1[:], x).then_inc(sm["s_xm"], 16)
            for i in range(2, PAIRS):
                sp.wait_ge(sm["s_w0lo"], i - 1)
                sp.dma_start(w0_in[i % 2], w0[:, :, i * PW:(i + 1) * PW]).then_inc(s_w0in[i], 16)
            sp.wait_ge(sm["s_hlo"], B * KT)
            sp.wait_ge(sm["s_xlo"], B)
            sp.dma_start(la[:], lora_a).then_inc(sm["s_lw"], 16)
            sp.dma_start(lb[:], lora_b).then_inc(sm["s_lw"], 16)
            sp.dma_start(wb_in[:], wbase).then_inc(sm["s_lw"], 16)
            for i in range(NP):
                if i >= 2:
                    sp.wait_ge(sm["s_pclo"], i - 1)
                sp.dma_start(piece[:, i % 2], w1_flat[:, i * PIECE:(i + 1) * PIECE]).then_inc(s_piece[i], 16)
                if i == 3:
                    sp.wait_ge(sm["s_const"], 1)
                    sp.dma_start(slot_rows.rearrange("(i p) w -> p i w", p=P),
                                 zrow[:].unsqueeze(1).to_broadcast([P, TILES, 2 * D])).then_inc(sm["s_zero"], 16)

            def load(i, par):
                sp.dma_start(rows[:, par], slot_rows[bass.ds(i * P, P), :]).then_inc(s_row[par], 16)

            def step(s, par):
                if known(s + 4):
                    sp.wait_ge(sm["s_ra"], s + 3)
                    load(s + 4, par)
                if known(s - 1):
                    sp.wait_ge(sm["s_ry"], s)
                    sp.dma_start(slot_out[bass.ds((s - 1) * P, P), :], yb[:, 1 - par]).then_inc(s_yst[1 - par], 16)

            sp.wait_ge(sm["s_scat"], 16 * K_TOP * NT)
            load(0, 0)
            load(1, 1)
            run_tiles(sp, step, 4)

            for b in range(B):
                sp.wait_ge(sm["s_acc"], (UN - B + b + 1) * TPB)
                sp.wait_ge(sm["s_cmb"], (b + 1) * TPB * K_TOP)
                sp.dma_start(out[:, b * TPB:(b + 1) * TPB], x1[:, b * TPB:(b + 1) * TPB]).then_inc(sm["s_out"], 16)
            sp.wait_ge(sm["s_out"], 16 * B)

        @block.gpsimd
        def _(pool):
            done = [0]

            def link(ins):
                done[0] += 1
                ins.then_inc(sm["s_pool"], 1)
                pool.wait_ge(sm["s_pool"], done[0])

            link(nc.gpsimd.memset(ident[:], 0.0))
            link(nc.gpsimd.affine_select(out=ident[:], in_=ident[:], compare_op=ALU.not_equal, fill=1.0, base=0,
                                         pattern=[[-1, P]], channel_multiplier=1))
            nc.gpsimd.memset(zrow[:], 0.0)
            nc.gpsimd.iota(rank_e[:], [[-1, E]], base=E, channel_multiplier=0, allow_small_or_imprecise_dtypes=True)
            nc.gpsimd.iota(tile_no[:], [[1, TILES], [0, E]], base=0, channel_multiplier=0,
                           allow_small_or_imprecise_dtypes=True)
            nc.gpsimd.memset(scan[:], 0.0)
            nc.gpsimd.memset(sel16[:], 0.0)
            link(nc.gpsimd.memset(ones16[:], 1.0))
            nc.gpsimd.affine_select(out=ident16[:], in_=ones16[:], compare_op=ALU.is_equal, fill=0.0, base=0,
                                    pattern=[[-1, P]], channel_multiplier=1)
            nc.gpsimd.affine_select(out=before[:], in_=ones16[:], compare_op=ALU.is_gt, fill=0.0, base=0,
                                    pattern=[[1, P]], channel_multiplier=-1).then_inc(sm["s_const"], 1)

            def x_lo(c):
                pool.wait_ge(sm["s_xsc"], c + 1)
                nc.gpsimd.tensor_tensor(chunk(c, LO), x_in[:, c % 2].rearrange("p k (t n) -> p k t n", n=P),
                                        chunk(c, HI), ALU.subtract).then_inc(sm["s_xlo"], 1)

            for c in range(B):
                x_lo(c)
            for j in range(PAIRS):
                pool.wait_ge(sm["s_w0sc"], j + 1)
                nc.gpsimd.tensor_tensor(w0s[:, LO, :, j * PW:(j + 1) * PW], w0_in[j % 2],
                                        w0s[:, HI, :, j * PW:(j + 1) * PW], ALU.subtract).then_inc(sm["s_w0lo"], 1)
            for i in range(NP):
                pool.wait_ge(sm["s_pcsc"], i + 1)
                nc.gpsimd.tensor_tensor(w1s[:, LO, i * PIECE:(i + 1) * PIECE], piece[:, i % 2],
                                        w1s[:, HI, i * PIECE:(i + 1) * PIECE], ALU.subtract).then_inc(sm["s_pclo"], 1)
            pool.wait_ge(sm["s_zero"], 16)
            pool.wait_ge(sm["s_idx"], 1)
            pool.wait_ge(sm["s_rows"], NT)
            for t in range(NT):
                for k in range(K_TOP):
                    pool.indirect_dma_start(slot_rows, bass.IndirectOffsetOnAxis(idx[:, k, t:t + 1], 0),
                                            xs[:, t].rearrange("p a k n -> p (a k n)"), None).then_inc(sm["s_scat"], 16)
            pool.wait_ge(s_yst[0], 16 * ((TILES + 1) // 2))
            pool.wait_ge(s_yst[1], 16 * (TILES // 2))
            for t in range(NT):
                if t >= 4:
                    pool.wait_ge(sm["s_cmb"], (t - 3) * K_TOP)
                for k in range(K_TOP):
                    pool.indirect_dma_start(yg[:, t % 4, k], None, slot_out,
                                            bass.IndirectOffsetOnAxis(idx[:, k, t:t + 1], 0)).then_inc(s_yg[t % 4], 16)

        @block.scalar
        def _(act):
            def h_hi(layer, c):
                for o in range(KT):
                    i = layer * B * KT + c * KT + o
                    act.wait_ge(sm["s_h"], i + 1)
                    nc.scalar.activation(hs[:, HI, o, c * S:(c + 1) * S], bank[4 + i % 2][:], ACT.Identity,
                                         bias=b_sc[:, layer, o:o + 1]).then_inc(sm["s_hhi"], 1)

            def x_hi(c):
                act.wait_ge(s_xin[c], 16)
                nc.scalar.activation(chunk(c, HI), x_in[:, c % 2].rearrange("p k (t n) -> p k t n", n=P), ACT.Copy,
                                     scale=SX).then_inc(sm["s_xhi"], 1)
                act.wait_ge(sm["s_xhi"], c + 1)
                nc.scalar.activation(x_in[:, c % 2], x_in[:, c % 2], ACT.Copy, scale=SX).then_inc(sm["s_xsc"], 1)

            def wb_hi(b):
                act.wait_ge(sm["s_wacc"], b + 1)
                nc.scalar.activation(flat(wbs[:, b, HI]), wacc[:, b], ACT.Copy).then_inc(sm["s_wbhi"], 1)

            def w0_hi(j):
                act.wait_ge(s_w0in[j], 16)
                nc.scalar.activation(w0s[:, HI, :, j * PW:(j + 1) * PW], w0_in[j % 2], ACT.Copy,
                                     scale=SW).then_inc(sm["s_w0hi"], 1)
                act.wait_ge(sm["s_w0hi"], j + 1)
                nc.scalar.activation(w0_in[j % 2], w0_in[j % 2], ACT.Copy, scale=SW).then_inc(sm["s_w0sc"], 1)

            act.dma_start(b_in[:, 0], bias0).then_inc(sm["s_small"], 16)
            act.dma_start(b_in[:, 1], bias1).then_inc(sm["s_small"], 16)
            act.dma_start(rin[:, 0], router).then_inc(sm["s_small"], 16)
            act.dma_start(rin[:, 1], gate).then_inc(sm["s_small"], 16)
            act.dma_start(ercol[:], cond_er).then_inc(sm["s_small"], 16)
            act.wait_ge(sm["s_small"], SMALL)
            act.wait_ge(sm["s_pool"], 2)
            for g in range(G):
                for b in range(2):
                    nc.scalar.activation(diag[:, b, g], ident[:], ACT.Copy,
                                         scale=ycol[:, (2 + b) * G + g:(2 + b) * G + g + 1]).then_inc(sm["s_diag"], 1)
            nc.scalar.activation(rs[:, :, HI], rin[:], ACT.Copy, scale=SW).then_inc(sm["s_rsp"], 1)
            x_hi(0)
            x_hi(1)
            wb_hi(0)
            wb_hi(1)
            x_hi(2)
            h_hi(0, 0)
            wb_hi(2)
            h_hi(0, 1)
            wb_hi(3)
            x_hi(3)
            w0_hi(0)
            h_hi(0, 2)
            w0_hi(1)
            h_hi(0, 3)
            nc.scalar.activation(exp_warm[:], ident[0:1, 0:1], ACT.Exp)

            def exps(layer):
                scale = 1.0 / (SH0 * SW) if layer == 0 else 1.0 / (SH1 * SW)
                act.wait_ge(sm["s_exq"], layer + 1)
                nc.scalar.activation(ex[:], ex[:], ACT.Exp, scale=scale).then_inc(sm["s_exp"], 1)

            exps(0)
            w0_hi(2)
            w0_hi(3)
            act.wait_ge(sm["s_xm"], 16)
            act.wait_ge(sm["s_r0"], 1)

            def add_bias(t):
                nc.scalar.activation(x1[:, t], x1[:, t], ACT.Identity, bias=BIAS[:, t:t + 1]).then_inc(sm["s_bias"], 1)

            def tr_hi(t):
                act.wait_ge(sm["s_tr"], t + 1)
                nc.scalar.activation(xs[:, t, HI], bank[6][:, 0:D].rearrange("p (k n) -> p k n", k=KT), ACT.Copy,
                                     scale=SX).then_inc(sm["s_trhi"], 1)

            def copy_rows(c):
                for t in range(c * TPB, (c + 1) * TPB):
                    act.wait_ge(sm["s_rt"], t + 1)
                    nc.scalar.activation(xs[:, t].rearrange("p a k n -> p (a k n)"), bank16[4 + t % 2][:, 0:2 * D],
                                         ACT.Copy).then_inc(sm["s_rows"], 1)

            add_bias(0)
            add_bias(1)
            for t in range(NT):
                if t + 2 < NT:
                    add_bias(t + 2)
                act.wait_ge(s_piece[t], 16)
                nc.scalar.activation(w1s[:, HI, t * PIECE:(t + 1) * PIECE], piece[:, t % 2], ACT.Copy,
                                     scale=SW).then_inc(sm["s_pchi"], 1)
                act.wait_ge(sm["s_pchi"], t + 1)
                nc.scalar.activation(piece[:, t % 2], piece[:, t % 2], ACT.Copy, scale=SW).then_inc(sm["s_pcsc"], 1)
                if t >= 1:
                    tr_hi(t - 1)
                if 1 <= t <= B:
                    b = t - 1
                    act.wait_ge(sm["s_wlf"], b + 1)
                    nc.scalar.activation(flat(wls[:, b, HI]), wl[:, b % 2], ACT.Copy).then_inc(sm["s_wlhi"], 1)
                if t > TPB and t % TPB == 1:
                    h_hi(1, t // TPB - 1)
                if t > TPB and t % TPB == 3:
                    copy_rows(t // TPB - 1)
            tr_hi(NT - 1)
            h_hi(1, B - 1)
            nc.scalar.activation(exp_warm[:], ident[0:1, 0:1], ACT.Exp)
            exps(1)
            copy_rows(B - 1)

            def shared_act(i):
                u, f = i // FT, i % FT
                M = FS[f]
                act.wait_ge(sm["s_gu"], i + 1)
                if i >= 2:
                    act.wait_ge(sm["s_prod"], i - 1)
                nc.scalar.activation(sil[0:M, i % 2], bank[2 * (i % 2)][0:M], ACT.Silu,
                                     scale=1.0 / (SH1 * SW)).then_inc(sm["s_sil"], 1)
                act.wait_ge(sm["s_prod"], i + 1)
                if f == 0 and u >= 2:
                    act.wait_ge(sm["s_dn"], (u - 1) * TPB)
                nc.scalar.activation(acts[0:M, u % 2, f, HI], prod[0:M, i % 2], ACT.Copy).then_inc(sm["s_ahi"], 1)

            for i in range(B * FT):
                shared_act(i)

            def step(s, par):
                i, q = s + 1, 1 - par
                if known(i):
                    act.wait_ge(sm["s_rg"], i + 1)
                    if again(i):
                        act.wait_ge(sm["s_rprod"], i - 1)
                    nc.scalar.activation(sil[:, q, 0:F], bank[2 * q][:, 0:F], ACT.Silu,
                                         scale=1.0 / (SH1 * SW)).then_inc(sm["s_rsil"], 1)
                    act.wait_ge(sm["s_rprod"], i + 1)
                    if again(i):
                        act.wait_ge(sm["s_rc"], i - 1)
                    nc.scalar.activation(ract[:, q, HI], prod[:, q, 0:F], ACT.Copy).then_inc(sm["s_rhi"], 1)
                i = s - 1
                if known(i):
                    act.wait_ge(sm["s_rd"], i + 1)
                    if again(i):
                        act.wait_ge(s_yst[q], landed(i - 2, q))
                    nc.scalar.activation(yb[:, q], bank[6 + q][:, 0:D], ACT.Copy).then_inc(sm["s_ry"], 1)

            act.wait_ge(sm["s_prod"], B * FT)
            run_tiles(act, step, 1)
            act.wait_ge(sm["s_rprod"], TILES)
            for i in range(B * FT, UN * FT):
                shared_act(i)

        @block.vector
        def _(dve):
            done = [0]

            def link(ins):
                done[0] += 1
                ins.then_inc(sm["s_dve"], 1)
                dve.wait_ge(sm["s_dve"], done[0])

            def h_lo(layer, c):
                for o in range(KT):
                    i = layer * B * KT + c * KT + o
                    dve.wait_ge(sm["s_hhi"], i + 1)
                    nc.vector.scalar_tensor_tensor(hs[:, LO, o, c * S:(c + 1) * S], bank[4 + i % 2][:],
                                                   b_sc[:, layer, o:o + 1], hs[:, HI, o, c * S:(c + 1) * S],
                                                   ALU.add, ALU.subtract).then_inc(sm["s_hlo"], 1)

            def masked(b):
                src = wacc[:, b] if b < 2 else bank[4 + b][:]
                if b == 2:
                    dve.wait_ge(sm["s_wbp"], 1)
                nc.vector.scalar_tensor_tensor(wacc[:, b], src, SWB, mask_in[:], ALU.mult,
                                               ALU.mult).then_inc(sm["s_wacc"], 1)

            def wb_lo(b):
                dve.wait_ge(sm["s_wbhi"], b + 1)
                nc.vector.tensor_tensor(flat(wbs[:, b, LO]), wacc[:, b], flat(wbs[:, b, HI]),
                                        ALU.subtract).then_inc(sm["s_wblo"], 1)

            dve.wait_ge(sm["s_small"], SMALL)
            link(nc.vector.tensor_scalar(b_sc[:, 0], b_in[:, 0], SH0, None, ALU.mult))
            nc.vector.tensor_scalar(b_sc[:, 1], b_in[:, 1], SH1, None, ALU.mult).then_inc(sm["s_bsc"], 1)
            for g in range(G):
                if g % 2 == 0:
                    dve.wait_ge(s_wc[g // 2], 16)
                for b in range(2):
                    y = ycol[:, b * G + g:b * G + g + 1]
                    if g == 0:
                        ins = nc.vector.tensor_scalar(wacc[:, b], wc_in[:, g], y, None, ALU.mult)
                    else:
                        dve.wait_ge(sm["s_dve"], done[0] - 1)
                        ins = nc.vector.scalar_tensor_tensor(wacc[:, b], wc_in[:, g], y, wacc[:, b], ALU.mult, ALU.add)
                    ins.then_inc(sm["s_dve"], 1)
                    done[0] += 1
            dve.wait_ge(sm["s_dve"], done[0])
            dve.wait_ge(sm["s_mask"], 16)
            masked(0)
            masked(1)
            wb_lo(0)
            dve.wait_ge(sm["s_rsp"], 1)
            nc.vector.scalar_tensor_tensor(rs[:, :, LO].rearrange("p a k e -> p a (k e)"),
                                           rin[:].rearrange("p a k e -> p a (k e)"), SW,
                                           rs[:, :, HI].rearrange("p a k e -> p a (k e)"),
                                           ALU.mult, ALU.subtract).then_inc(sm["s_rsp"], 1)
            masked(2)
            wb_lo(1)
            masked(3)
            h_lo(0, 0)
            wb_lo(2)
            h_lo(0, 1)
            wb_lo(3)
            h_lo(0, 2)
            h_lo(0, 3)

            def each(a):
                return a.unsqueeze(2).to_broadcast([P, NT, E])

            def per_expert(a):
                return a.unsqueeze(1).to_broadcast([P, NT, E])

            def top(src, best, onehot, after=None):
                link(nc.vector.tensor_reduce(best, src, AX.X, ALU.max))
                if after is not None:
                    after()
                link(nc.vector.tensor_tensor(t1[:], src, each(best), ALU.is_equal))
                link(nc.vector.tensor_tensor(t1[:], t1[:], per_expert(rank_e[:]), ALU.mult))
                link(nc.vector.tensor_reduce(K1, t1[:], AX.X, ALU.max))
                link(nc.vector.tensor_tensor(onehot[:], t1[:], each(K1), ALU.is_equal))

            def route(layer):
                lg = bank[6 + layer][:, 0:NT * E].rearrange("p (t e) -> p t e", t=NT)
                dve.wait_ge(sm["s_log"], layer + 1)
                if layer == 0:
                    dve.wait_ge(sm["s_const"], 1)
                top(lg, M1, oh1, lambda: nc.vector.tensor_tensor(ex[:], lg, each(M1), ALU.subtract)
                    .then_inc(sm["s_exq"], 1))
                link(nc.vector.scalar_tensor_tensor(t2[:], oh1[:], -FAR, lg, ALU.mult, ALU.add))
                top(t2[:], M2, oh2)
                link(nc.vector.tensor_tensor(t1[:], oh1[:], oh2[:], ALU.add))
                if layer == 1:
                    nc.vector.tensor_copy(sel16[:, NT:], t1[:]).then_inc(sm["s_sel"], 1)
                dve.wait_ge(sm["s_exp"], layer + 1)
                link(nc.vector.tensor_tensor(t1[:], ex[:], t1[:], ALU.mult))
                link(nc.vector.tensor_reduce(S2, t1[:], AX.X, ALU.add))
                if layer == 0:
                    link(nc.vector.tensor_reduce(SUM, ex[:], AX.X, ALU.add))
                    link(nc.vector.scalar_tensor_tensor(S2, SUM, EPS_TOPK, S2, ALU.mult, ALU.add))
                    link(nc.vector.reciprocal(REC, S2))
                    link(nc.vector.tensor_tensor(coef[:], t1[:], each(REC), ALU.mult))
                    link(nc.vector.tensor_tensor(t1[:], t1[:], coef[:], ALU.mult))
                    link(nc.vector.tensor_reduce(S2, t1[:], AX.X, ALU.add))
                    link(nc.vector.reciprocal(SUM, SUM))
                    nc.vector.tensor_tensor(BIAS, S2, SUM, ALU.mult).then_inc(sm["s_r0"], 1)
                    link(nc.vector.tensor_scalar(coef[:], coef[:], 1.0 / (SH0 * SW), None, ALU.mult))
                else:
                    link(nc.vector.reciprocal(REC, S2))
                    link(nc.vector.tensor_scalar(REC, REC, 1.0 / (SA * SW), None, ALU.mult))
                    link(nc.vector.tensor_tensor(coef[:], t1[:], each(REC), ALU.mult))

            route(0)

            def tr_lo(t):
                dve.wait_ge(sm["s_trhi"], t + 1)
                nc.vector.scalar_tensor_tensor(xs[:, t, LO], bank[6][:, 0:D].rearrange("p (k n) -> p k n", k=KT),
                                               SX, xs[:, t, HI], ALU.mult, ALU.subtract).then_inc(sm["s_trlo"], 1)

            for t in range(NT):
                if t < B:
                    if t == 0:
                        dve.wait_ge(sm["s_lw"], 48)
                    if t >= 2:
                        dve.wait_ge(sm["s_lora"], t - 1)
                    nc.vector.tensor_scalar(lbw[:, t % 2], lb[:], ercol[:, t:t + 1], LORA_SCALE * SWC, ALU.mult,
                                            ALU.mult).then_inc(sm["s_lbw"], 1)
                dve.wait_ge(sm["s_bias"], t + 1)
                for j in range(PAIRS):
                    dve.wait_ge(sm["s_ffn"], t * PAIRS + j + 1)
                    for h in range(2):
                        e = 2 * j + h
                        if e:
                            dve.wait_ge(sm["s_comb"], t * E + e)
                        nc.vector.scalar_tensor_tensor(x1[:, t], bank[j][:, h * D:(h + 1) * D], coef[:, t, e:e + 1],
                                                       x1[:, t], ALU.mult, ALU.add).then_inc(sm["s_comb"], 1)
                if t >= 1:
                    tr_lo(t - 1)
                if 1 <= t <= B:
                    b = t - 1
                    dve.wait_ge(sm["s_lora"], b + 1)
                    if b >= 2:
                        dve.wait_ge(sm["s_wllo"], b - 1)
                    nc.vector.scalar_tensor_tensor(wl[:, b % 2], wb_in[:], SWC, bank[7][:], ALU.mult,
                                                   ALU.add).then_inc(sm["s_wlf"], 1)
                    dve.wait_ge(sm["s_wlhi"], b + 1)
                    nc.vector.tensor_tensor(flat(wls[:, b, LO]), wl[:, b % 2], flat(wls[:, b, HI]),
                                            ALU.subtract).then_inc(sm["s_wllo"], 1)
                if t > TPB and t % TPB == 1:
                    h_lo(1, t // TPB - 1)
            tr_lo(NT - 1)
            h_lo(1, B - 1)
            route(1)

            def slots():
                rank = bank[6][:, 0:NT * E].rearrange("p (t e) -> p t e", t=NT)
                dve.wait_ge(sm["s_rank"], 1)
                link(nc.vector.tensor_scalar(cnt[:], bank[6][:, NT * E:NT * E + E], float(P - 1), None, ALU.add))
                link(nc.vector.tensor_scalar(cnt[:], cnt[:], 7, None, ALU.arith_shift_right))
                link(nc.vector.tensor_copy(scan[:, 0, PAD:], cnt[:]))
                for i, d in enumerate((1, 2, 4)):
                    a, b = scan[:, i % 2], scan[:, (i + 1) % 2]
                    link(nc.vector.tensor_tensor(b[:, PAD:], a[:, PAD:], a[:, PAD - d:PAD - d + E], ALU.add))
                upto = scan[:, 1, PAD:]
                link(nc.vector.tensor_tensor(base[:], upto, cnt[:], ALU.subtract))
                link(nc.vector.scalar_tensor_tensor(t2[:], per_expert(base[:]), float(P), rank, ALU.mult, ALU.add))
                link(nc.vector.tensor_tensor(t1[:], oh1[:], t2[:], ALU.mult))
                link(nc.vector.tensor_reduce(W1, t1[:], AX.X, ALU.add))
                link(nc.vector.tensor_tensor(t1[:], oh2[:], t2[:], ALU.mult))
                link(nc.vector.tensor_reduce(W2, t1[:], AX.X, ALU.add))
                nc.vector.tensor_copy(idx[:], st[:, 7:9]).then_inc(sm["s_idx"], 1)
                link(nc.vector.tensor_tensor(tile_no[:], tile_no[:],
                                             scan[0:1, 1, PAD:].unsqueeze(1).to_broadcast([1, TILES, E]), ALU.is_ge))
                link(nc.vector.tensor_reduce(tef[:], tile_no[:], AX.X, ALU.add))
                link(nc.vector.tensor_scalar(tef[:], tef[:], float(E - 1), float(WE), ALU.min, ALU.mult))
                link(nc.vector.tensor_scalar(te[:], tef[:], float(SHARED * WE), None, ALU.add))
                for n, first_tile in enumerate((2, 3, 5, 6)):
                    tiles = te[:, first_tile:first_tile + 2 * LOOPS - 1:2]
                    ins = nc.vector.tensor_copy(te4[:, :, n], tiles)
                ins.then_inc(sm["s_idx"], 1)
                for k, (oh, w) in enumerate(((oh1, W1), (oh2, W2))):
                    link(nc.vector.tensor_tensor(t1[:], oh[:], coef[:], ALU.mult))
                    link(nc.vector.tensor_reduce(w, t1[:], AX.X, ALU.add))

            def shared_dve(i):
                u, f = i // FT, i % FT
                M = FS[f]
                dve.wait_ge(sm["s_sil"], i + 1)
                if i >= 2:
                    dve.wait_ge(sm["s_alo"], i - 1)
                    dve.wait_ge(sm["s_ahi"], i - 1)
                nc.vector.scalar_tensor_tensor(prod[0:M, i % 2], bank[2 * (i % 2) + 1][0:M],
                                               SA / (SH1 * SW), sil[0:M, i % 2], ALU.mult,
                                               ALU.mult).then_inc(sm["s_prod"], 1)
                dve.wait_ge(sm["s_ahi"], i + 1)
                nc.vector.tensor_tensor(acts[0:M, u % 2, f, LO], prod[0:M, i % 2], acts[0:M, u % 2, f, HI],
                                        ALU.subtract).then_inc(sm["s_alo"], 1)

            def accumulate(u):
                for q in range(TPB):
                    i = u * TPB + q
                    t = (u % B) * TPB + q
                    dve.wait_ge(sm["s_dn"], i + 1)
                    nc.vector.scalar_tensor_tensor(x1[:, t], bank[4 + i % 2][:, 0:D], 1.0 / (SA * SW), x1[:, t],
                                                   ALU.mult, ALU.add).then_inc(sm["s_acc"], 1)

            def combine(c):
                for t in range(c * TPB, (c + 1) * TPB):
                    dve.wait_ge(s_yg[t % 4], 16 * K_TOP * (t // 4 + 1))
                    for k, w in enumerate((W1, W2)):
                        if k:
                            dve.wait_ge(sm["s_cmb"], t * K_TOP + k)
                        nc.vector.scalar_tensor_tensor(x1[:, t], yg[:, t % 4, k], w[:, t:t + 1], x1[:, t],
                                                       ALU.mult, ALU.add).then_inc(sm["s_cmb"], 1)

            for i in range(B * FT):
                shared_dve(i)
                if i == 1:
                    slots()
                if i >= FT and i % FT == 1:
                    accumulate(i // FT - 1)
            accumulate(B - 1)

            def step(s, par):
                i, q = s - 1, 1 - par
                if known(i):
                    dve.wait_ge(sm["s_rc"], i + 1)
                    if again(i):
                        dve.wait_ge(sm["s_rd"], i - 1)
                    n = FT - 1
                    nc.vector.tensor_copy(aT[:, q, 0:n].rearrange("p f a n -> p (f a n)").bitcast(F32),
                                          bank[5][:, 0:n * P])
                    nc.vector.tensor_copy(aT[0:FS[n], q, n].rearrange("p a n -> p (a n)").bitcast(F32),
                                          bank[5][0:FS[n], n * P:FT * P]).then_inc(sm["s_rcx"], 1)
                i = s + 2
                if known(i):
                    dve.wait_ge(sm["s_ra"], i + 1)
                    if again(i):
                        dve.wait_ge(sm["s_ru"], i - 1)
                    nc.vector.tensor_copy(rT[:, par].rearrange("p a k n -> p (a k n)").bitcast(F32),
                                          bank[4][:, 0:D]).then_inc(sm["s_rx"], 1)
                i = s + 1
                if known(i):
                    dve.wait_ge(sm["s_ru"], i + 1)
                    dve.wait_ge(sm["s_rsil"], i + 1)
                    nc.vector.scalar_tensor_tensor(prod[:, q, 0:F], bank[2 * q + 1][:, 0:F], SA / (SH1 * SW),
                                                   sil[:, q, 0:F], ALU.mult, ALU.mult).then_inc(sm["s_rprod"], 1)
                    dve.wait_ge(sm["s_rhi"], i + 1)
                    nc.vector.tensor_tensor(ract[:, q, LO], prod[:, q, 0:F], ract[:, q, HI],
                                            ALU.subtract).then_inc(sm["s_rlo"], 1)

            dve.wait_ge(sm["s_ahi"], B * FT)
            run_tiles(dve, step, 2)

            for i in range(B * FT, UN * FT):
                shared_dve(i)
                if i % FT == 1:
                    u = i // FT - 1
                    if u >= B:
                        accumulate(u)
                        combine(u % B)
            combine(B - 1)
            accumulate(UN - 1)

        @block.tensor
        def _(pe):
            def group(out_ap, terms, s=None):
                for i, (l, r) in enumerate(terms):
                    mm = nc.tensor.matmul(out_ap, l, r, start=(i == 0), stop=(i == len(terms) - 1))
                if s is not None:
                    mm.then_inc(sm[s], 1)
                return mm

            for g in range(G):
                if g % 2 == 0:
                    pe.wait_ge(s_wc[g // 2], 16)
                for b in range(2):
                    pe.wait_ge(sm["s_diag"], 2 * g + b + 1)
                    mm = nc.tensor.matmul(bank[6 + b][:], diag[:, b, g], wc_in[:, g], start=(g == 0), stop=(g == G - 1))
            mm.then_inc(sm["s_wbp"], 1)

            def project(layer, c):
                w = wbs if layer == 0 else wls
                for o in range(KT):
                    i = layer * B * KT + c * KT + o
                    if i >= 2:
                        pe.wait_ge(sm["s_hlo"], i - 1)
                    group(bank[4 + i % 2][:].rearrange("p (t n) -> p t n", n=P),
                          [(w[:, c, a, k, o * P:(o + 1) * P], xs[:, c * TPB:(c + 1) * TPB, b, k])
                           for k in range(KT) for a, b in PASSES], "s_h")

            def logits(layer, c):
                pe.wait_ge(sm["s_hlo"], (layer * B + c + 1) * KT)
                for t in range(c * TPB, (c + 1) * TPB):
                    mm = group(bank[6 + layer][:, t * E:(t + 1) * E],
                               [(hs[:, a, k, t * P:(t + 1) * P], rs[:, layer, b, k, :])
                                for k in range(KT) for a, b in PASSES])
                if c == B - 1:
                    mm.then_inc(sm["s_log"], 1)

            for c in range(B):
                pe.wait_ge(sm["s_xlo"], c + 1)
                pe.wait_ge(sm["s_wblo"], c + 1)
                project(0, c)
                if c >= 1:
                    if c == 1:
                        pe.wait_ge(sm["s_rsp"], 2)
                        pe.wait_ge(sm["s_wacc"], 3)
                    logits(0, c - 1)
            logits(0, B - 1)

            def transposes(t):
                pe.wait_ge(sm["s_comb"], (t + 1) * E)
                if t >= 1:
                    pe.wait_ge(sm["s_trlo"], t)
                for k in range(KT):
                    mm = nc.tensor.transpose(bank[6][:, k * P:(k + 1) * P], x1[:, t, k * P:(k + 1) * P], ident[:])
                mm.then_inc(sm["s_tr"], 1)

            def token_rows(c):
                for t in range(c * TPB, (c + 1) * TPB):
                    if t >= c * TPB + 2:
                        pe.wait_ge(sm["s_rows"], t - 1)
                    for a in range(2):
                        for k in range(KT):
                            o = (a * KT + k) * P
                            mm = nc.tensor.transpose(bank16[4 + t % 2][:, o:o + P], hs[:, a, k, t * P:(t + 1) * P],
                                                     ident16[:])
                    mm.then_inc(sm["s_rt"], 1)

            def layer1_input(c):
                pe.wait_ge(sm["s_trlo"], (c + 1) * TPB)
                pe.wait_ge(sm["s_wllo"], c + 1)
                if c >= 1:
                    pe.wait_ge(sm["s_rows"], c * TPB)
                project(1, c)

            for t in range(NT):
                for j in range(PAIRS):
                    if t == 0:
                        pe.wait_ge(sm["s_w0lo"], j + 1)
                    else:
                        pe.wait_ge(sm["s_comb"], (t - 1) * E + 2 * j + 2)
                    group(bank[j][:], [(hs[:, a, k, t * P:(t + 1) * P], w0s[:, b, k, j * PW:(j + 1) * PW])
                                       for k in range(KT) for a, b in PASSES], "s_ffn")
                if t >= 1:
                    transposes(t - 1)
                if 1 <= t <= B:
                    b = t - 1
                    pe.wait_ge(sm["s_lbw"], b + 1)
                    if b >= 1:
                        pe.wait_ge(sm["s_wlf"], b)
                    for k in range(KT):
                        mm = nc.tensor.matmul(bank[7][:, k * D:(k + 1) * D], la[:, k * P:(k + 1) * P], lbw[:, b % 2],
                                              start=True, stop=True)
                    mm.then_inc(sm["s_lora"], 1)
                if t > TPB:
                    c = t // TPB - 1
                    if t % TPB == 1:
                        layer1_input(c)
                    if t % TPB == 2:
                        logits(1, c)
                    if t % TPB == 3:
                        token_rows(c)
            transposes(NT - 1)
            layer1_input(B - 1)
            logits(1, B - 1)
            token_rows(B - 1)

            def down(u):
                e = u // B
                pe.wait_ge(sm["s_alo"], (u + 1) * FT)
                for q in range(TPB):
                    i = u * TPB + q
                    if i >= 2:
                        pe.wait_ge(sm["s_acc"], i - 1)
                    group(bank[4 + i % 2][:, 0:D], [(acts[0:FS[f], u % 2, f, a, q * P:(q + 1) * P], w_dn(b, e, f))
                                                    for f in range(FT) for a, b in PASSES], "s_dn")

            def gate_up(i):
                u, f = i // FT, i % FT
                c, e = u % B, u // B
                if i >= 2:
                    pe.wait_ge(sm["s_prod"], i - 1)
                for g in range(2):
                    mm = group(bank[2 * (i % 2) + g][0:FS[f]], [(w_gu(a, e, k, g, f), hs[:, b, k, c * S:(c + 1) * S])
                                                               for k in range(KT) for a, b in PASSES])
                mm.then_inc(sm["s_gu"], 1)

            def ranks():
                pe.wait_ge(sm["s_sel"], 1)
                sel = sel16[:].rearrange("p t e -> p (t e)")
                nc.tensor.matmul(bank[6][:, 0:NT * E], before[:], sel[:, NT * E:], start=True, stop=False)
                for d in range(1, NT):
                    nc.tensor.matmul(bank[6][:, 0:NT * E], ones16[:], sel[:, (NT - d) * E:(2 * NT - d) * E],
                                     start=False, stop=(d == NT - 1))
                for t in range(NT, 2 * NT):
                    mm = nc.tensor.matmul(bank[6][:, NT * E:NT * E + E], ones16[:], sel[:, t * E:(t + 1) * E],
                                          start=(t == NT), stop=(t == 2 * NT - 1))
                mm.then_inc(sm["s_rank"], 1)

            pe.wait_ge(sm["s_pclo"], NP)
            pe.wait_ge(sm["s_rows"], NT)
            for i in range(B * FT):
                gate_up(i)
                if i == 1:
                    ranks()
                if i >= FT and i % FT == 1:
                    down(i // FT - 1)
            down(B - 1)

            def experts(ap):
                return nc.values_load_multi_w_load_instructions(
                    ap, engines=(nc.tensor.engine,), min_val=SHARED * WE, max_val=(NEXP - 1) * WE,
                    skip_runtime_bounds_check_because="the table's entries are clamped where it is made")[1]

            def step(s, par, down_at, gate_at):
                q = 1 - par
                i = s + 2
                if known(i):
                    pe.wait_ge(s_row[par], landed(i, par))
                    if isinstance(i, int) and i == 1:
                        pe.wait_ge(sm["s_rx"], i)
                    for a in range(2):
                        for k in range(KT):
                            o = (a * KT + k) * P
                            mm = nc.tensor.transpose(bank16[4][:, o:o + P], rows[:, par, o:o + P], ident16[:])
                    mm.then_inc(sm["s_ra"], 1)
                i = s - 1
                if known(i):
                    pe.wait_ge(sm["s_rcx"], i + 1)
                    if again(i):
                        pe.wait_ge(sm["s_ry"], i - 1)
                    group(bank[6 + q][:, 0:D],
                          [(aT[0:FS[f], q, f, a], w1s[0:FS[f], b, bass.ds(down_at + (KT * 2 * F + f * D), D)])
                           for f in range(FT) for a, b in PASSES], "s_rd")
                i = s
                if known(i):
                    pe.wait_ge(sm["s_rlo"], i + 1)
                    for f in range(FT):
                        for a in range(2):
                            o = (2 * f + a) * P
                            mm = nc.tensor.transpose(bank16[5][0:FS[f], o:o + P],
                                                     ract[:, par, a, f * P:f * P + FS[f]], ident16[:])
                    mm.then_inc(sm["s_rc"], 1)
                i = s + 2
                if known(i):
                    pe.wait_ge(sm["s_rx"], i + 1)
                    for g, done in enumerate(("s_rg", "s_ru")):
                        group(bank[2 * par + g][:, 0:F],
                              [(rT[:, par, a, k], w1s[:, b, bass.ds(gate_at + (k * 2 + g) * F, F)])
                               for k in range(KT) for a, b in PASSES], done)

            pe.wait_ge(sm["s_acc"], B * TPB)
            pe.wait_ge(sm["s_idx"], 2)

            def single(s, par):
                down_at = experts(te[0:1, s - 1:s])[0] if known(s - 1) else None
                gate_at = experts(te[0:1, s + 2:s + 3])[0] if known(s + 2) else None
                step(s, par, down_at, gate_at)

            for s in range(-2, 3):
                single(s, s % 2)
            with pe.Fori(0, LOOPS) as j:
                a, b, c, d = experts(te4[0:1, bass.ds(j, 1), :].rearrange("p a b -> p (a b)"))
                step(j * 2 + 3, 1, a, c)
                step(j * 2 + 4, 0, b, d)
            for s in range(3 + 2 * LOOPS, TILES + 1):
                single(s, s % 2)

            pe.wait_ge(sm["s_rcx"], TILES)
            pe.wait_ge(sm["s_rprod"], TILES)
            for i in range(B * FT, UN * FT):
                gate_up(i)
                if i % FT == 1 and i // FT - 1 >= B:
                    down(i // FT - 1)
            down(UN - 1)


def kernel(x, cond_8, L0_cond_weight, L0_cond_mask, L0_cond_bias, L0_ffn_router_w, L0_ffn_expert_weights,
           L1_cond_W_base, L1_cond_b_base, L1_cond_As, L1_cond_Bs, L1_ffn_gate_w, L1_ffn_exp_gate,
           L1_ffn_exp_up, L1_ffn_exp_down, L1_ffn_sh_gate, L1_ffn_sh_up, L1_ffn_sh_down):
    import numpy as np
    import concourse.bacc as bacc
    from concourse.bass_utils import run_bass_kernel_spmd

    Bb, S, D = x.shape
    N, KT = Bb * S, D // P
    E, R, _ = L1_cond_As.shape
    F = L1_ffn_exp_gate.shape[2]

    def by_k(a):
        return np.ascontiguousarray(a.reshape(KT, P, -1).transpose(1, 0, 2))

    def swiglu_rows(wg, wu, wd):
        n = wg.shape[0]
        gu = np.concatenate([wg, wu], axis=2).reshape(n, KT, P, 2 * F).transpose(2, 0, 1, 3).reshape(P, n, -1)
        ft = -(-F // P)
        dn = np.zeros((n, ft * P, D), wd.dtype)
        dn[:, :F] = wd
        dn = dn.reshape(n, ft, P, D).transpose(2, 0, 1, 3).reshape(P, n, -1)
        return np.concatenate([gu, dn], axis=2)

    x = np.asarray(x)
    tok = x.reshape(N, D)
    c = np.asarray
    ins = {
        "cond_row": c(cond_8).reshape(1, -1),
        "cond_er": np.ascontiguousarray(np.repeat(c(cond_8).T, R, axis=0)),
        "xT": by_k(tok.T),
        "x": np.ascontiguousarray(tok.reshape(N // P, P, D).transpose(1, 0, 2)),
        "wc": np.ascontiguousarray(c(L0_cond_weight).reshape(E, D, KT, P).transpose(3, 0, 2, 1).reshape(P, E, KT * D)),
        "mask": by_k(c(L0_cond_mask).T).reshape(P, KT * D),
        "bias0": np.ascontiguousarray(c(L0_cond_bias).reshape(KT, P).T),
        "router": by_k(c(L0_ffn_router_w).T),
        "w0": by_k(c(L0_ffn_expert_weights).transpose(1, 0, 2).reshape(D, E * D)),
        "wbase": by_k(c(L1_cond_W_base).T).reshape(P, KT * D),
        "bias1": np.ascontiguousarray(c(L1_cond_b_base).reshape(KT, P).T),
        "lora_a": c(L1_cond_As).reshape(E * R, D),
        "lora_b": np.ascontiguousarray(c(L1_cond_Bs).transpose(0, 2, 1).reshape(E * R, D)),
        "gate": by_k(c(L1_ffn_gate_w)),
        "w1": np.ascontiguousarray(np.concatenate(
            [swiglu_rows(c(L1_ffn_sh_gate), c(L1_ffn_sh_up), c(L1_ffn_sh_down)),
             swiglu_rows(c(L1_ffn_exp_gate), c(L1_ffn_exp_up), c(L1_ffn_exp_down))], axis=1)),
    }
    nc = bacc.Bacc("TRN2", target_bir_lowering=False, num_devices=1)
    aps = {n: nc.dram_tensor(n, a.shape, mybir.dt.from_np(a.dtype), kind="ExternalInput").ap()
           for n, a in ins.items()}
    out = nc.dram_tensor("out", (P, N // P, D), F32, kind="ExternalOutput").ap()
    build_program(nc, out=out, **aps)
    r = run_bass_kernel_spmd(nc, [ins], core_ids=[0])
    return r.results[0]["out"].reshape(P, N // P, D).transpose(1, 0, 2).reshape(Bb, S, D)
```

```python
from contextlib import ExitStack

import concourse.bass as bass
from concourse import mybir

ALU = mybir.AluOpType
ACT = mybir.ActivationFunctionType
AX = mybir.AxisListType
F32 = mybir.dt.float32
F16 = mybir.dt.float16
I32 = mybir.dt.int32

P = 128
HI, LO = 0, 1
PASSES = ((HI, HI), (LO, HI), (HI, LO))

SWB = 64.0
SH0 = SWB
SX = 8.0
SW = 64.0
SWC = 32.0
SH1 = SX * SWC
SA = 512.0
LORA_SCALE = 2.0
EPS_TOPK = 1e-6
FAR = 1e30


def build_program(nc, cond_row, cond_er, xT, x, wc, mask, bias0, router, w0, wbase, bias1, lora_a, lora_b,
                  gate, w1, out):
    _, KT, N = xT.shape
    D = KT * P
    B = cond_er.shape[1]
    G = wc.shape[1]
    E = gate.shape[2]
    S = N // B
    NT = N // P
    TPB = S // P
    PAIRS = E // 2
    PW = 2 * D
    NEXP, WE = w1.shape[1:]
    FT = 3
    F = (WE - FT * D) // (2 * KT)
    FS = [min(P, F - P * f) for f in range(FT)]
    SHARED = NEXP - E
    FLAT = NEXP * WE
    NP = NT
    PIECE = FLAT // NP
    K_TOP = 2
    TILES = (N * K_TOP + E * (P - 1)) // P
    PAD = E // 2
    LOOPS = (TILES - 5) // 2
    TWO = NT // 2
    SF = SHARED * F
    REST = SF % P
    ST = SF // P + 1
    SR = [P] * (ST - 1) + [REST]
    EARLY = 3 * ST
    DOWN = {ST + 1: 0, EARLY - 1: 1, EARLY + 1: 2}
    WARM = 9
    SCALED = {EARLY + 1: (0, 1), EARLY + 3: (2,), B * ST - 1: (3,)}
    G2 = G - 2
    ROW = 2 * D + 2
    w1_flat = w1.rearrange("p e w -> p (e w)")
    slot_rows = nc.dram_tensor("slot_rows", (TILES * P, ROW), F16).ap()
    results = nc.dram_tensor("results", (P + K_TOP * N, D), F32).ap()

    with ExitStack() as ctx:
        def sb(name, shape, dt, where=ctx):
            return where.enter_context(nc.sbuf_tensor(name, shape, dt))

        def sem(name):
            return ctx.enter_context(nc.semaphore(name))

        def flat(ap):
            return ap.rearrange("p a b -> p (a b)")

        xrow = sb("xrow", [P, NT, ROW], F16)
        hs = sb("hs", [P, 2, KT, N], F16)
        x1 = sb("x1", [P, NT, D], F32)
        w1s = sb("w1s", [P, 2, FLAT], F16)
        wls = sb("wls", [P, B, 2, KT, D], F16)
        rs = sb("rs", [P, 2, 2, KT, E], F16)
        rin = sb("rin", [P, 2, KT, E], F32)
        ycol = sb("ycol", [P, B * G], F32)
        ercol = sb("ercol", [P, B], F32)
        b_in = sb("b_in", [P, 2, KT], F32)
        b_sc = sb("b_sc", [P, 2, KT], F32)
        ident = sb("ident", [P, P], F32)
        ident16 = sb("ident16", [P, P], F16)
        before = sb("before", [P, P], F16)
        ones16 = sb("ones16", [P, P], F16)
        zrow = sb("zrow", [P, ROW], F16)
        rank_e = sb("rank_e", [P, E], F32)
        tile_no = sb("tile_no", [1, TILES, E], F32)
        t1 = sb("t1", [P, NT, E], F32)
        t2 = sb("t2", [P, NT, E], F32)
        lg = sb("lg", [P, NT, E], F32)
        ex = sb("ex", [P, NT, E], F32)
        oh1 = sb("oh1", [P, NT, E], F32)
        oh2 = sb("oh2", [P, NT, E], F32)
        coef = sb("coef", [P, NT, E], F32)
        sel16 = sb("sel16", [P, 2 * NT, E], F16)
        st = sb("st", [P, 9, NT], F32)
        M1, K1, M2, SUM, S2, REC, BIAS, W1, W2 = (st[:, i, :] for i in range(9))
        cnt = sb("cnt", [P, E], I32)
        scan = sb("scan", [P, 2, PAD + E], F32)
        base = sb("base", [P, E], F32)
        idx = sb("idx", [P, 2, NT], I32)
        tef = sb("tef", [1, TILES], F32)
        te = sb("te", [1, TILES], I32)
        te4 = sb("te4", [1, LOOPS, 4], I32)
        exp_warm = sb("exp_warm", [1, 1], F32)
        warm = sb("warm", [P, 512], F16)

        xs = xrow[:, :, 0:2 * D].rearrange("p t (a k n) -> p t a k n", a=2, k=KT)
        place = xrow[:, :, 2 * D:ROW].bitcast(I32)

        l0 = ExitStack()
        w0s = sb("w0s", [P, 2, KT, E * D], F16, l0)
        first = ExitStack()
        wbs = sb("wbs", [P, B, 2, KT, D], F16, first)
        mask_in = sb("mask_in", [P, KT * D], F32, first)
        wacc = sb("wacc", [P, B, KT * D], F32, first)
        first.close()
        second = ExitStack()
        piece = sb("piece", [P, 2, PIECE], F32, second)
        la = sb("la", [P, D], F32, second)
        lb = sb("lb", [P, D], F32, second)
        lbw = sb("lbw", [P, 2, D], F32, second)
        wb_in = sb("wb_in", [P, KT * D], F32, second)
        wl = sb("wl", [P, 2, KT * D], F32, second)
        second.close()
        l0.close()
        sil = sb("sil", [P, 2, S], F32)
        prod = sb("prod", [P, 2, S], F32)
        rows = sb("rows", [P, 2, ROW], F16)
        rT = sb("rT", [P, 2, 2, KT, P], F16)
        ract = sb("ract", [P, 2, 2, F], F16)
        aT = sb("aT", [P, 2, FT, 2, P], F16)
        yb = sb("yb", [P, 2, D], F32)
        yg0 = sb("yg0", [P, K_TOP, TPB, D], F32)
        acts = sb("acts", [P, 2, ST, 2, S], F16)
        ids = sb("ids", [P, 2], I32)

        wc_in = x1[:].rearrange("p a b -> p (a b)").rearrange("p (g w) -> p g w", g=G)
        w0_in = [w1s[:, hl, FLAT - (n + 1) * 2 * KT * PW:FLAT - n * 2 * KT * PW].bitcast(F32)
                 .rearrange("p (k w) -> p k w", k=KT) for hl in range(2) for n in range(2)]
        x_in = [w1s[:, hl, FLAT - 4 * KT * PW - (n + 1) * 2 * KT * S:FLAT - 4 * KT * PW - n * 2 * KT * S].bitcast(F32)
                .rearrange("p (k w) -> p k w", k=KT) for hl in range(2) for n in range(2)]
        YW = 2 * K_TOP * TPB * D
        yg = [yg0[:]] + [w1s[:, HI, FLAT - (n + 1) * YW:FLAT - n * YW].bitcast(F32)
                         .rearrange("p (k t d) -> p k t d", k=K_TOP, t=TPB) for n in range(B - 1)]
        diag_at = FLAT - 4 * KT * PW - 4 * KT * S - 2 * 2 * G * P
        diag = w1s[:, HI, diag_at:diag_at + 2 * 2 * G * P].bitcast(F32).rearrange("p (b g m) -> p b g m", b=2, g=G)

        bank = [ctx.enter_context(nc.psum_tensor(f"bank{i}", [P, 512], F32)) for i in range(8)]
        bank16 = [b[:].bitcast(F16) for b in bank]

        names = (
            "s_y",
            "s_mask",
            "s_small",
            "s_xm",
            "s_lw",
            "s_zero",
            "s_const",
            "s_pool",
            "s_dve",
            "s_warm",
            "s_diag",
            "s_wbp",
            "s_wacc",
            "s_wbhi",
            "s_wblo",
            "s_xhi",
            "s_xlo",
            "s_rsp",
            "s_bsc",
            "s_h",
            "s_hhi",
            "s_hlo",
            "s_w0hi",
            "s_w0sc",
            "s_w0lo",
            "s_log",
            "s_lg",
            "s_exq",
            "s_exp",
            "s_r0",
            "s_bias",
            "s_ffn",
            "s_comb",
            "s_pchi",
            "s_pcsc",
            "s_pclo",
            "s_lbw",
            "s_lora",
            "s_wlf",
            "s_wlhi",
            "s_wllo",
            "s_tr",
            "s_trhi",
            "s_trlo",
            "s_rt",
            "s_rows",
            "s_sel",
            "s_rank",
            "s_idx",
            "s_scat",
            "s_gu",
            "s_sil",
            "s_prod",
            "s_ahi",
            "s_alo",
            "s_dn",
            "s_acc",
            "s_ra",
            "s_rx",
            "s_rg",
            "s_ru",
            "s_rsil",
            "s_rprod",
            "s_rhi",
            "s_rlo",
            "s_rc",
            "s_rcx",
            "s_rd",
            "s_ry",
            "s_w1",
            "s_scaled",
            "s_add1",
            "s_cmb",
            "s_out",
        )
        sm = {n: sem(n) for n in names}
        s_wc = [sem(f"s_wc{c}") for c in range(4)]
        s_xin = [sem(f"s_xin{c}") for c in range(B)]
        s_w0in = [sem(f"s_w0in{c}") for c in range(PAIRS)]
        s_piece = [sem(f"s_piece{c}") for c in range(NP)]
        s_row = [sem(f"s_row{c}") for c in range(2)]
        s_ids = [sem(f"s_ids{c}") for c in range(2)]
        s_put = [sem(f"s_put{c}") for c in range(2)]
        s_yg = [sem(f"s_yg{c}") for c in range(B)]
        SMALL = 16 * 5
        block = ctx.enter_context(nc.Block())

        def w_gu(hl, k, g, f):
            full = SF - REST
            o = k * 2 * SF + (g * full + f * P if f < ST - 1 else 2 * full)
            return w1s[:, hl, o:o + (P if f < ST - 1 else 2 * REST)]

        def w_dn(hl, f):
            o = KT * 2 * SF + f * D
            return w1s[0:SR[f], hl, o:o + D]

        def chunk(c, hl):
            return xs[:, c * TPB:(c + 1) * TPB, hl].rearrange("p t k n -> p k t n")

        def side(i):
            return (i + i // EARLY) % 2

        def h_bank(i):
            return bank[(i + 4) % 6 if i < B * KT else 4 + i % 2]

        def turned():
            return bank[6][:, 0:2 * D].rearrange("p (t k n) -> p t k n", t=2, k=KT)

        def known(i):
            return not isinstance(i, int) or 0 <= i < TILES

        def again(i):
            return not isinstance(i, int) or i >= 2

        def landed(i, par):
            return i * 8 + (16 - 8 * par)

        def run_tiles(eng, step, ahead):
            for s in range(-2, 3):
                step(s, s % 2)
            pairs = (TILES - 3 - ahead) // 2
            with eng.Fori(0, pairs) as j:
                step(j * 2 + 3, 1)
                step(j * 2 + 4, 0)
            for s in range(3 + 2 * pairs, TILES + 1):
                step(s, s % 2)

        @block.sync
        def _(sp):
            sp.dma_start(ycol[:], cond_row.partition_broadcast(P).rearrange("p a n -> p (a n)")).then_inc(sm["s_y"], 16)
            for i in range(4):
                sp.dma_start(wc_in[:, 2 * i:2 * i + 2, :], wc[:, 2 * i:2 * i + 2, :]).then_inc(s_wc[i], 16)
            sp.dma_start(mask_in[:], mask).then_inc(sm["s_mask"], 16)
            sp.dma_start(b_in[:, 0], bias0).then_inc(sm["s_small"], 16)
            sp.dma_start(b_in[:, 1], bias1).then_inc(sm["s_small"], 16)
            sp.dma_start(rin[:, 0], router).then_inc(sm["s_small"], 16)
            sp.dma_start(rin[:, 1], gate).then_inc(sm["s_small"], 16)
            sp.dma_start(ercol[:], cond_er).then_inc(sm["s_small"], 16)
            for c in range(B):
                sp.dma_start(x_in[c], xT[:, :, c * S:(c + 1) * S]).then_inc(s_xin[c], 16)
            for c in range(B):
                sp.dma_start(w0_in[c], w0[:, :, c * PW:(c + 1) * PW]).then_inc(s_w0in[c], 16)
            sp.wait_ge(sm["s_wacc"], 3)
            sp.wait_ge(sm["s_wbp"], 1)
            sp.dma_start(x1[:], x).then_inc(sm["s_xm"], 16)
            sp.wait_ge(sm["s_h"], B * KT)
            sp.dma_start(la[:], lora_a).then_inc(sm["s_lw"], 16)
            sp.dma_start(lb[:], lora_b).then_inc(sm["s_lw"], 16)
            sp.dma_start(wb_in[:], wbase).then_inc(sm["s_lw"], 16)
            for i in range(NP):
                if i >= 2:
                    sp.wait_ge(sm["s_pclo"], i - 1)
                sp.dma_start(piece[:, i % 2], w1_flat[:, i * PIECE:(i + 1) * PIECE]).then_inc(s_piece[i], 16)
                if i == 0:
                    sp.wait_ge(sm["s_const"], 1)
                if i >= 2:
                    first, end = ((i + n - 2) * TILES // (NP - 2) for n in range(2))
                    sp.dma_start(slot_rows[first * P:end * P, :].rearrange("(i p) w -> p i w", p=P),
                                 zrow[:].unsqueeze(1).to_broadcast([P, end - first, ROW])).then_inc(sm["s_zero"], 16)

            def load(i, par):
                sp.dma_start(rows[:, par], slot_rows[bass.ds(i * P, P), :]).then_inc(s_row[par], 16)

            def step(s, par):
                if known(s + 4):
                    sp.wait_ge(sm["s_ra"], s + 3)
                    load(s + 4, par)
                if known(s):
                    if again(s):
                        sp.wait_ge(s_put[par], landed(s - 2, par))
                    sp.dma_start(ids[:, par:par + 1].bitcast(F16),
                                 slot_rows[bass.ds(s * P, P), 2 * D:ROW]).then_inc(s_ids[par], 16)

            sp.wait_ge(sm["s_scat"], 16 * K_TOP * NT)
            load(0, 0)
            load(1, 1)
            run_tiles(sp, step, 4)

            sp.wait_ge(s_put[0], 16 * ((TILES + 1) // 2))
            sp.wait_ge(s_put[1], 16 * (TILES // 2))
            for c in range(B):
                for k in range(K_TOP):
                    at = P + k * N + c * S
                    sp.dma_start(yg[c][:, k], results[at:at + S, :].rearrange("(t p) d -> p t d", p=P)
                                 ).then_inc(s_yg[c], 16)
            for t in range(0, NT, 2):
                sp.wait_ge(sm["s_acc"], t + 2)
                sp.wait_ge(sm["s_cmb"], t + 2)
                sp.dma_start(out[:, t:t + 2], x1[:, t:t + 2]).then_inc(sm["s_out"], 16)
            sp.wait_ge(sm["s_out"], 16 * TWO)

        @block.gpsimd
        def _(pool):
            done = [0]

            def link(ins):
                done[0] += 1
                ins.then_inc(sm["s_pool"], 1)
                pool.wait_ge(sm["s_pool"], done[0])

            link(nc.gpsimd.memset(ident[:], 0.0))
            link(nc.gpsimd.affine_select(out=ident[:], in_=ident[:], compare_op=ALU.not_equal, fill=1.0, base=0,
                                         pattern=[[-1, P]], channel_multiplier=1))
            nc.gpsimd.memset(zrow[:, 0:2 * D], 0.0)
            nc.gpsimd.iota(zrow[:, 2 * D:ROW].bitcast(I32), [[0, 1]], base=0, channel_multiplier=1)
            nc.gpsimd.iota(place, [[P, NT], [0, 1]], base=P, channel_multiplier=1)
            nc.gpsimd.iota(rank_e[:], [[-1, E]], base=E, channel_multiplier=0, allow_small_or_imprecise_dtypes=True)
            nc.gpsimd.iota(tile_no[:], [[1, TILES], [0, E]], base=0, channel_multiplier=0,
                           allow_small_or_imprecise_dtypes=True)
            nc.gpsimd.memset(scan[:], 0.0)
            nc.gpsimd.memset(sel16[:], 0.0)
            link(nc.gpsimd.memset(ones16[:], 1.0))
            nc.gpsimd.affine_select(out=ident16[:], in_=ones16[:], compare_op=ALU.is_equal, fill=0.0, base=0,
                                    pattern=[[-1, P]], channel_multiplier=1)
            nc.gpsimd.affine_select(out=before[:], in_=ones16[:], compare_op=ALU.is_gt, fill=0.0, base=0,
                                    pattern=[[1, P]], channel_multiplier=-1).then_inc(sm["s_const"], 1)

            def x_lo(c):
                pool.wait_ge(sm["s_xhi"], c + 1)
                nc.gpsimd.tensor_tensor(chunk(c, LO), x_in[c].rearrange("p k (t n) -> p k t n", n=P),
                                        chunk(c, HI), ALU.subtract).then_inc(sm["s_xlo"], 1)

            for c in range(B):
                x_lo(c)
            for j in range(PAIRS):
                pool.wait_ge(sm["s_w0sc"], j + 1)
                nc.gpsimd.tensor_tensor(w0s[:, LO, :, j * PW:(j + 1) * PW], w0_in[j],
                                        w0s[:, HI, :, j * PW:(j + 1) * PW], ALU.subtract).then_inc(sm["s_w0lo"], 1)
            for i in range(NP):
                pool.wait_ge(sm["s_pcsc"], i + 1)
                nc.gpsimd.tensor_tensor(w1s[:, LO, i * PIECE:(i + 1) * PIECE], piece[:, i % 2],
                                        w1s[:, HI, i * PIECE:(i + 1) * PIECE], ALU.subtract).then_inc(sm["s_pclo"], 1)
            pool.wait_ge(sm["s_zero"], 16 * (NP - 2))
            pool.wait_ge(sm["s_idx"], 1)
            for k in range(K_TOP):
                if k:
                    pool.wait_ge(sm["s_scat"], 16 * NT)
                    link(nc.gpsimd.iota(place, [[P, NT], [0, 1]], base=P + N, channel_multiplier=1))
                for t in range(NT):
                    if not k:
                        pool.wait_ge(sm["s_rows"], t + 1)
                    pool.indirect_dma_start(slot_rows, bass.IndirectOffsetOnAxis(idx[:, k, t:t + 1], 0),
                                            xrow[:, t], None).then_inc(sm["s_scat"], 16)

            for i in range(TILES):
                q = i % 2
                if i >= 1:
                    pool.wait_ge(s_put[1 - q], landed(i - 1, 1 - q))
                pool.wait_ge(s_ids[q], landed(i, q))
                pool.wait_ge(sm["s_ry"], i + 1)
                pool.indirect_dma_start(results, bass.IndirectOffsetOnAxis(ids[:, q:q + 1], 0),
                                        yb[:, q], None).then_inc(s_put[q], 16)

            for t in range(NT):
                c, q = t // TPB, t % TPB
                if t % TPB == 0 and c != B - 1:
                    pool.wait_ge(sm["s_acc"], (c + 1) * TPB)
                pool.wait_ge(sm["s_scaled"], t + 1)
                nc.gpsimd.tensor_tensor(x1[:, t], x1[:, t], yg[c][:, 0, q], ALU.add).then_inc(sm["s_add1"], 1)

        @block.scalar
        def _(act):
            def h_hi(layer, c):
                act.wait_ge(sm["s_bsc"], 1)
                for o in range(KT):
                    i = layer * B * KT + c * KT + o
                    act.wait_ge(sm["s_h"], i + 1)
                    nc.scalar.activation(hs[:, HI, o, c * S:(c + 1) * S], h_bank(i)[:], ACT.Identity,
                                         bias=b_sc[:, layer, o:o + 1]).then_inc(sm["s_hhi"], 1)

            def x_hi(c):
                act.wait_ge(s_xin[c], 16)
                nc.scalar.activation(chunk(c, HI), x_in[c].rearrange("p k (t n) -> p k t n", n=P),
                                     ACT.Copy).then_inc(sm["s_xhi"], 1)

            def wb_hi(b):
                act.wait_ge(sm["s_wacc"], b + 1)
                nc.scalar.activation(flat(wbs[:, b, HI]), wacc[:, b], ACT.Copy).then_inc(sm["s_wbhi"], 1)

            def w0_hi(j):
                act.wait_ge(s_w0in[j], 16)
                nc.scalar.activation(w0s[:, HI, :, j * PW:(j + 1) * PW], w0_in[j], ACT.Copy,
                                     scale=SW).then_inc(sm["s_w0hi"], 1)
                act.wait_ge(sm["s_w0hi"], j + 1)
                nc.scalar.activation(w0_in[j], w0_in[j], ACT.Copy, scale=SW).then_inc(sm["s_w0sc"], 1)

            act.wait_ge(sm["s_y"], 16)
            act.wait_ge(sm["s_pool"], 2)
            for g in range(G):
                for b in range(2):
                    nc.scalar.activation(diag[:, b, g], ident[:], ACT.Copy,
                                         scale=ycol[:, (2 + b) * G + g:(2 + b) * G + g + 1]).then_inc(sm["s_diag"], 1)
            act.wait_ge(sm["s_small"], SMALL)
            nc.scalar.activation(rs[:, :, HI], rin[:], ACT.Copy, scale=SW).then_inc(sm["s_rsp"], 1)
            x_hi(0)
            x_hi(1)
            wb_hi(0)
            wb_hi(1)
            x_hi(2)
            x_hi(3)
            wb_hi(2)
            h_hi(0, 0)
            wb_hi(3)
            w0_hi(0)
            h_hi(0, 1)
            w0_hi(1)
            h_hi(0, 2)
            w0_hi(2)
            h_hi(0, 3)
            nc.scalar.activation(exp_warm[:], ident[0:1, 0:1], ACT.Exp)

            def exps(n, tiles, scale):
                act.wait_ge(sm["s_exq"], n + 1)
                nc.scalar.activation(ex[:, tiles], ex[:, tiles], ACT.Exp, scale=scale).then_inc(sm["s_exp"], 1)

            exps(0, slice(0, NT // 2), 1.0 / (SH0 * SW))
            w0_hi(3)
            act.wait_ge(sm["s_xm"], 16)

            def add_bias(t):
                nc.scalar.activation(x1[:, t], x1[:, t], ACT.Identity, bias=BIAS[:, t:t + 1]).then_inc(sm["s_bias"], 1)

            def tr_hi(m):
                act.wait_ge(sm["s_tr"], m + 1)
                nc.scalar.activation(xs[:, 2 * m:2 * m + 2, HI], turned(), ACT.Copy, scale=SX).then_inc(sm["s_trhi"], 1)

            def copy_rows(c, tiles=(0, TPB - 1)):
                for t in range(c * TPB + tiles[0], c * TPB + tiles[1] + 1):
                    act.wait_ge(sm["s_rt"], t + 1)
                    nc.scalar.activation(xrow[:, t, 0:2 * D], bank16[4 + t % 2][:, 0:2 * D],
                                         ACT.Copy).then_inc(sm["s_rows"], 1)

            def split_piece(i):
                act.wait_ge(s_piece[i], 16)
                nc.scalar.activation(w1s[:, HI, i * PIECE:(i + 1) * PIECE], piece[:, i % 2], ACT.Copy,
                                     scale=SW).then_inc(sm["s_pchi"], 1)
                act.wait_ge(sm["s_pchi"], i + 1)
                nc.scalar.activation(piece[:, i % 2], piece[:, i % 2], ACT.Copy, scale=SW).then_inc(sm["s_pcsc"], 1)

            def wl_hi(b):
                act.wait_ge(sm["s_wlf"], b + 1)
                nc.scalar.activation(flat(wls[:, b, HI]), wl[:, b % 2], ACT.Copy).then_inc(sm["s_wlhi"], 1)

            for m in range(TWO):
                if m == 1:
                    exps(1, slice(NT // 2, NT), 1.0 / (SH0 * SW))
                if m >= 3 and m % 2 == 1:
                    h_hi(1, (m - 3) // 2)
                split_piece(2 * m)
                if m >= 1:
                    tr_hi(m - 1)
                if m < B:
                    wl_hi(m)
                if m == 0:
                    act.wait_ge(sm["s_comb"], 2 * E)
                    act.wait_ge(sm["s_r0"], 1)
                    add_bias(0)
                    add_bias(1)
                if m == 3:
                    act.wait_ge(sm["s_r0"], 2)
                if m + 1 < TWO:
                    add_bias(2 * m + 2)
                    add_bias(2 * m + 3)
                if m >= 3 and m % 2 == 1:
                    copy_rows((m - 3) // 2)
                split_piece(2 * m + 1)

            def shared_act(i):
                c, f, p = i // ST, i % ST, side(i)
                M = SR[f]
                gate = bank[2 * p][0:P] if f < ST - 1 else bank[2 * p][REST:2 * REST]
                if i == 0:
                    tr_hi(TWO - 1)
                act.wait_ge(sm["s_gu"], i + 1)
                if i >= 2:
                    act.wait_ge(sm["s_prod"], i - 1)
                nc.scalar.activation(sil[0:M, p], gate, ACT.Silu, scale=1.0 / (SH1 * SW)).then_inc(sm["s_sil"], 1)
                if i == 1:
                    h_hi(1, B - 1)
                if i == 3:
                    copy_rows(B - 1, (0, 1))
                if i == 4:
                    copy_rows(B - 1, (2, 3))
                act.wait_ge(sm["s_prod"], i + 1)
                if f == 0 and c >= 2:
                    act.wait_ge(sm["s_dn"], (c - 1) * TPB)
                nc.scalar.activation(acts[0:M, c % 2, f, HI], prod[0:M, p], ACT.Copy).then_inc(sm["s_ahi"], 1)

            for i in range(EARLY):
                shared_act(i)
                if i == ST + 1:
                    exps(2, slice(0, NT), 1.0 / (SH1 * SW))

            def step(s, par):
                i, q = s + 1, 1 - par
                if known(i):
                    act.wait_ge(sm["s_rg"], i + 1)
                    if again(i):
                        act.wait_ge(sm["s_rprod"], i - 1)
                    nc.scalar.activation(sil[:, q, 0:F], bank[2 * q][:, 0:F], ACT.Silu,
                                         scale=1.0 / (SH1 * SW)).then_inc(sm["s_rsil"], 1)
                    act.wait_ge(sm["s_rprod"], i + 1)
                    if again(i):
                        act.wait_ge(sm["s_rc"], i - 1)
                    nc.scalar.activation(ract[:, q, HI], prod[:, q, 0:F], ACT.Copy).then_inc(sm["s_rhi"], 1)
                i = s - 1
                if known(i):
                    act.wait_ge(sm["s_rd"], i + 1)
                    if again(i):
                        act.wait_ge(s_put[q], landed(i - 2, q))
                    nc.scalar.activation(yb[:, q], bank[6 + q][:, 0:D], ACT.Copy).then_inc(sm["s_ry"], 1)

            act.wait_ge(sm["s_prod"], EARLY)
            run_tiles(act, step, 1)
            act.wait_ge(sm["s_rprod"], TILES)
            for i in range(EARLY, B * ST):
                shared_act(i)
                for c in SCALED.get(i, ()):
                    act.wait_ge(s_yg[c], 16 * K_TOP)
                    act.wait_ge(sm["s_w1"], 1)
                    for t in range(c * TPB, (c + 1) * TPB):
                        y = yg[c][:, 0, t % TPB]
                        nc.scalar.activation(y, y, ACT.Copy, scale=W1[:, t:t + 1]).then_inc(sm["s_scaled"], 1)

        @block.vector
        def _(dve):
            done = [0]

            def link(ins):
                done[0] += 1
                ins.then_inc(sm["s_dve"], 1)
                dve.wait_ge(sm["s_dve"], done[0])

            def h_lo(layer, c):
                for o in range(KT):
                    i = layer * B * KT + c * KT + o
                    dve.wait_ge(sm["s_hhi"], i + 1)
                    nc.vector.scalar_tensor_tensor(hs[:, LO, o, c * S:(c + 1) * S], h_bank(i)[:],
                                                   b_sc[:, layer, o:o + 1], hs[:, HI, o, c * S:(c + 1) * S],
                                                   ALU.add, ALU.subtract).then_inc(sm["s_hlo"], 1)

            def masked(b):
                src = bank[7][:] if b == 3 else wacc[:, b]
                nc.vector.scalar_tensor_tensor(wacc[:, b], src, SWB, mask_in[:], ALU.mult,
                                               ALU.mult).then_inc(sm["s_wacc"], 1)

            def wb_lo(b):
                dve.wait_ge(sm["s_wbhi"], b + 1)
                nc.vector.tensor_tensor(flat(wbs[:, b, LO]), wacc[:, b], flat(wbs[:, b, HI]),
                                        ALU.subtract).then_inc(sm["s_wblo"], 1)

            nc.vector.memset(warm[:], 0.0).then_inc(sm["s_warm"], 1)
            dve.wait_ge(sm["s_y"], 16)
            for g in range(G):
                if g % 2 == 0:
                    dve.wait_ge(s_wc[g // 2], 16)
                for b in range(2):
                    y = ycol[:, b * G + g:b * G + g + 1]
                    if g == 0:
                        ins = nc.vector.tensor_scalar(wacc[:, b], wc_in[:, g], y, None, ALU.mult)
                    else:
                        dve.wait_ge(sm["s_dve"], done[0] - 1)
                        ins = nc.vector.scalar_tensor_tensor(wacc[:, b], wc_in[:, g], y, wacc[:, b], ALU.mult, ALU.add)
                    ins.then_inc(sm["s_dve"], 1)
                    done[0] += 1
            dve.wait_ge(sm["s_dve"], done[0])
            dve.wait_ge(sm["s_mask"], 16)
            masked(0)
            masked(1)
            dve.wait_ge(sm["s_small"], SMALL)
            nc.vector.tensor_scalar(b_sc[:, 0], b_in[:, 0], SH0, None, ALU.mult)
            nc.vector.tensor_scalar(b_sc[:, 1], b_in[:, 1], SH1, None, ALU.mult).then_inc(sm["s_bsc"], 1)
            wb_lo(0)
            dve.wait_ge(sm["s_rsp"], 1)
            nc.vector.scalar_tensor_tensor(rs[:, :, LO].rearrange("p a k e -> p a (k e)"),
                                           rin[:].rearrange("p a k e -> p a (k e)"), SW,
                                           rs[:, :, HI].rearrange("p a k e -> p a (k e)"),
                                           ALU.mult, ALU.subtract).then_inc(sm["s_rsp"], 1)
            wb_lo(1)
            for g in range(G2, G):
                y = ycol[:, 2 * G + g:2 * G + g + 1]
                if g == G2:
                    link(nc.vector.tensor_scalar(wacc[:, 2], wc_in[:, g], y, None, ALU.mult))
                else:
                    link(nc.vector.scalar_tensor_tensor(wacc[:, 2], wc_in[:, g], y, wacc[:, 2], ALU.mult, ALU.add))
            dve.wait_ge(sm["s_wbp"], 1)
            link(nc.vector.tensor_tensor(wacc[:, 2], wacc[:, 2], bank[6][:], ALU.add))
            masked(2)
            masked(3)
            wb_lo(2)
            h_lo(0, 0)
            wb_lo(3)
            h_lo(0, 1)

            def each(a, tiles):
                return a[:, tiles].unsqueeze(2).to_broadcast([P, tiles.stop - tiles.start, E])

            def per_expert(a):
                return a.unsqueeze(1).to_broadcast([P, NT, E])

            def top(src, best, onehot, tiles):
                h = tiles.stop - tiles.start
                link(nc.vector.tensor_reduce(best[:, tiles], src, AX.X, ALU.max))
                link(nc.vector.tensor_tensor(t1[:, tiles], src, each(best, tiles), ALU.is_equal))
                link(nc.vector.tensor_tensor(t1[:, tiles], t1[:, tiles],
                                             rank_e[:].unsqueeze(1).to_broadcast([P, h, E]), ALU.mult))
                link(nc.vector.tensor_reduce(K1[:, tiles], t1[:, tiles], AX.X, ALU.max))
                link(nc.vector.tensor_tensor(onehot[:, tiles], t1[:, tiles], each(K1, tiles), ALU.is_equal))

            def largest(tiles):
                top(lg[:, tiles], M1, oh1, tiles)
                nc.vector.tensor_tensor(ex[:, tiles], lg[:, tiles], each(M1, tiles),
                                        ALU.subtract).then_inc(sm["s_exq"], 1)

            def second(tiles):
                link(nc.vector.scalar_tensor_tensor(t2[:, tiles], oh1[:, tiles], -FAR, lg[:, tiles], ALU.mult, ALU.add))
                top(t2[:, tiles], M2, oh2, tiles)
                link(nc.vector.tensor_tensor(t1[:, tiles], oh1[:, tiles], oh2[:, tiles], ALU.add))

            def shares0(half, tiles):
                dve.wait_ge(sm["s_exp"], half + 1)
                link(nc.vector.tensor_tensor(t1[:, tiles], ex[:, tiles], t1[:, tiles], ALU.mult))
                link(nc.vector.tensor_reduce(S2[:, tiles], t1[:, tiles], AX.X, ALU.add))
                link(nc.vector.tensor_reduce(SUM[:, tiles], ex[:, tiles], AX.X, ALU.add))
                link(nc.vector.scalar_tensor_tensor(S2[:, tiles], SUM[:, tiles], EPS_TOPK, S2[:, tiles], ALU.mult,
                                                    ALU.add))
                link(nc.vector.reciprocal(REC[:, tiles], S2[:, tiles]))
                link(nc.vector.tensor_scalar(REC[:, tiles], REC[:, tiles], 1.0 / (SH0 * SW), None, ALU.mult))
                link(nc.vector.tensor_tensor(coef[:, tiles], t1[:, tiles], each(REC, tiles), ALU.mult))
                link(nc.vector.tensor_tensor(t1[:, tiles], t1[:, tiles], coef[:, tiles], ALU.mult))
                link(nc.vector.tensor_reduce(S2[:, tiles], t1[:, tiles], AX.X, ALU.add))
                link(nc.vector.reciprocal(SUM[:, tiles], SUM[:, tiles]))
                nc.vector.scalar_tensor_tensor(BIAS[:, tiles], S2[:, tiles], SH0 * SW, SUM[:, tiles], ALU.mult,
                                               ALU.mult).then_inc(sm["s_r0"], 1)

            def take_logits(layer, half, tiles):
                dve.wait_ge(sm["s_log"], 4 if layer else half + 1)
                at = bank[6 + layer][:, tiles.start * E:tiles.stop * E].rearrange("p (t e) -> p t e", e=E)
                ins = nc.vector.tensor_copy(lg[:, tiles], at)
                ins.then_inc(sm["s_lg"], 1)
                dve.wait_ge(sm["s_lg"], 2 * layer + half + 1)

            HALVES = [slice(0, NT // 2), slice(NT // 2, NT)]
            ALL = slice(0, NT)
            dve.wait_ge(sm["s_const"], 1)
            take_logits(0, 0, HALVES[0])
            h_lo(0, 2)
            largest(HALVES[0])
            second(HALVES[0])
            shares0(0, HALVES[0])

            def tr_lo(m):
                dve.wait_ge(sm["s_trhi"], m + 1)
                nc.vector.scalar_tensor_tensor(xs[:, 2 * m:2 * m + 2, LO], turned(), SX, xs[:, 2 * m:2 * m + 2, HI],
                                               ALU.mult, ALU.subtract).then_inc(sm["s_trlo"], 1)

            def lora_scaled(b):
                if b >= 2:
                    dve.wait_ge(sm["s_lora"], b - 1)
                nc.vector.tensor_scalar(lbw[:, b % 2], lb[:], ercol[:, b:b + 1], LORA_SCALE * SWC, ALU.mult,
                                        ALU.mult).then_inc(sm["s_lbw"], 1)

            def wl_sum(b):
                dve.wait_ge(sm["s_lora"], b + 1)
                nc.vector.scalar_tensor_tensor(wl[:, b % 2], wb_in[:], SWC, bank[7][:], ALU.mult,
                                               ALU.add).then_inc(sm["s_wlf"], 1)
                if b + 1 < B:
                    lora_scaled(b + 1)

            def wl_lo(b):
                dve.wait_ge(sm["s_wlhi"], b + 1)
                nc.vector.tensor_tensor(flat(wls[:, b, LO]), wl[:, b % 2], flat(wls[:, b, HI]),
                                        ALU.subtract).then_inc(sm["s_wllo"], 1)

            dve.wait_ge(sm["s_lw"], 48)
            lora_scaled(0)
            for m in range(TWO):
                if m == 0:
                    dve.wait_ge(sm["s_xm"], 16)
                else:
                    dve.wait_ge(sm["s_bias"], 2 * m + 2)
                for j in range(PAIRS):
                    n = 2 * (m * PAIRS + j)
                    for h in range(2):
                        e = 2 * j + h
                        for a in range(2):
                            t = 2 * m + a
                            if h == 0:
                                dve.wait_ge(sm["s_ffn"], n + a + 1)
                            if e:
                                dve.wait_ge(sm["s_comb"], 2 * n + 2 * h + a - 1)
                            nc.vector.scalar_tensor_tensor(x1[:, t], bank[(n + a) % 4][:, h * D:(h + 1) * D],
                                                           coef[:, t, e:e + 1], x1[:, t], ALU.mult,
                                                           ALU.add).then_inc(sm["s_comb"], 1)
                    if m == 0 and j == 0:
                        h_lo(0, 3)
                    if j == 0 and m >= 3 and m % 2 == 1:
                        h_lo(1, (m - 3) // 2)
                    if j == 1 and m < B:
                        wl_sum(m)
                    if j == 2 and m >= 1:
                        tr_lo(m - 1)
                if m < B:
                    wl_lo(m)
                if m == 0:
                    take_logits(0, 1, HALVES[1])
                    largest(HALVES[1])
                if m == 1:
                    second(HALVES[1])
                if m == 2:
                    shares0(1, HALVES[1])

            def shares1():
                dve.wait_ge(sm["s_exp"], 3)
                link(nc.vector.tensor_tensor(t1[:], oh1[:], oh2[:], ALU.add))
                link(nc.vector.tensor_tensor(t1[:], ex[:], t1[:], ALU.mult))
                link(nc.vector.tensor_reduce(S2, t1[:], AX.X, ALU.add))
                link(nc.vector.reciprocal(REC, S2))
                link(nc.vector.tensor_scalar(REC, REC, 1.0 / (SA * SW), None, ALU.mult))
                link(nc.vector.tensor_tensor(coef[:], t1[:], each(REC, ALL), ALU.mult))
                link(nc.vector.tensor_tensor(t1[:], oh1[:], coef[:], ALU.mult))
                link(nc.vector.tensor_reduce(W1, t1[:], AX.X, ALU.add))
                link(nc.vector.tensor_tensor(t1[:], oh2[:], coef[:], ALU.mult))
                nc.vector.tensor_reduce(W2, t1[:], AX.X, ALU.add).then_inc(sm["s_w1"], 1)
                dve.wait_ge(sm["s_w1"], 1)

            def groups():
                dve.wait_ge(sm["s_rank"], 1)
                link(nc.vector.tensor_scalar(cnt[:], bank[6][:, NT * E:NT * E + E], float(P - 1), None, ALU.add))
                link(nc.vector.tensor_scalar(cnt[:], cnt[:], 7, None, ALU.arith_shift_right))
                link(nc.vector.tensor_copy(scan[:, 0, PAD:], cnt[:]))
                for i, d in enumerate((1, 2, 4)):
                    a, b = scan[:, i % 2], scan[:, (i + 1) % 2]
                    link(nc.vector.tensor_tensor(b[:, PAD:], a[:, PAD:], a[:, PAD - d:PAD - d + E], ALU.add))
                upto = scan[:, 1, PAD:]
                link(nc.vector.tensor_tensor(base[:], upto, cnt[:], ALU.subtract))

            def slots():
                rank = bank[6][:, 0:NT * E].rearrange("p (t e) -> p t e", t=NT)
                link(nc.vector.scalar_tensor_tensor(t2[:], per_expert(base[:]), float(P), rank, ALU.mult, ALU.add))
                link(nc.vector.tensor_tensor(t1[:], oh1[:], t2[:], ALU.mult))
                link(nc.vector.tensor_reduce(W1, t1[:], AX.X, ALU.add))
                link(nc.vector.tensor_tensor(t1[:], oh2[:], t2[:], ALU.mult))
                link(nc.vector.tensor_reduce(W2, t1[:], AX.X, ALU.add))
                nc.vector.tensor_copy(idx[:], st[:, 7:9]).then_inc(sm["s_idx"], 1)

            def tile_experts():
                link(nc.vector.tensor_tensor(tile_no[:], tile_no[:],
                                             scan[0:1, 1, PAD:].unsqueeze(1).to_broadcast([1, TILES, E]), ALU.is_ge))
                link(nc.vector.tensor_reduce(tef[:], tile_no[:], AX.X, ALU.add))
                link(nc.vector.tensor_scalar(tef[:], tef[:], float(E - 1), float(WE), ALU.min, ALU.mult))
                link(nc.vector.tensor_scalar(te[:], tef[:], float(SHARED * WE), None, ALU.add))
                for n, first_tile in enumerate((2, 3, 5, 6)):
                    tiles = te[:, first_tile:first_tile + 2 * LOOPS - 1:2]
                    ins = nc.vector.tensor_copy(te4[:, :, n], tiles)
                ins.then_inc(sm["s_idx"], 1)

            def combine(t):
                c, q = t // TPB, t % TPB
                dve.wait_ge(sm["s_add1"], t + 1)
                nc.vector.scalar_tensor_tensor(x1[:, t], yg[c][:, 1, q], W2[:, t:t + 1], x1[:, t],
                                               ALU.mult, ALU.add).then_inc(sm["s_cmb"], 1)

            def shared_dve(i):
                c, f, p = i // ST, i % ST, side(i)
                M = SR[f]
                up = bank[2 * p + 1][0:M] if f < ST - 1 else bank[2 * p][0:M]
                dve.wait_ge(sm["s_sil"], i + 1)
                if i >= 2:
                    dve.wait_ge(sm["s_alo"], i - 1)
                    dve.wait_ge(sm["s_ahi"], i - 1)
                nc.vector.scalar_tensor_tensor(prod[0:M, p], up, SA / (SH1 * SW), sil[0:M, p], ALU.mult,
                                               ALU.mult).then_inc(sm["s_prod"], 1)
                if i == 1:
                    h_lo(1, B - 1)
                dve.wait_ge(sm["s_ahi"], i + 1)
                nc.vector.tensor_tensor(acts[0:M, c % 2, f, LO], prod[0:M, p], acts[0:M, c % 2, f, HI],
                                        ALU.subtract).then_inc(sm["s_alo"], 1)

            def accumulate(c, tiles=()):
                if c == B - 1:
                    dve.wait_ge(sm["s_cmb"], NT)
                for q in range(TPB):
                    t = c * TPB + q
                    dve.wait_ge(sm["s_dn"], t + 1)
                    nc.vector.scalar_tensor_tensor(x1[:, t], bank[4 + q][:, 0:D], 1.0 / (SA * SW), x1[:, t],
                                                   ALU.mult, ALU.add).then_inc(sm["s_acc"], 1)
                    if tiles:
                        combine(tiles[q])

            tr_lo(TWO - 1)
            for i in range(EARLY):
                shared_dve(i)
                if i == 2:
                    take_logits(1, 0, ALL)
                    largest(ALL)
                    second(ALL)
                    nc.vector.tensor_copy(sel16[:, NT:], t1[:]).then_inc(sm["s_sel"], 1)
                if i == 4:
                    groups()
                if i == 5:
                    slots()
                if i == 6:
                    tile_experts()
                if i in DOWN:
                    accumulate(DOWN[i])

            def step(s, par):
                i, q = s - 1, 1 - par
                if known(i):
                    dve.wait_ge(sm["s_rc"], i + 1)
                    if again(i):
                        dve.wait_ge(sm["s_rd"], i - 1)
                    n = FT - 1
                    nc.vector.tensor_copy(aT[:, q, 0:n].rearrange("p f a n -> p (f a n)").bitcast(F32),
                                          bank[5][:, 0:n * P])
                    nc.vector.tensor_copy(aT[0:FS[n], q, n].rearrange("p a n -> p (a n)").bitcast(F32),
                                          bank[5][0:FS[n], n * P:FT * P]).then_inc(sm["s_rcx"], 1)
                i = s + 2
                if known(i):
                    dve.wait_ge(sm["s_ra"], i + 1)
                    if again(i):
                        dve.wait_ge(sm["s_ru"], i - 1)
                    nc.vector.tensor_copy(rT[:, par].rearrange("p a k n -> p (a k n)").bitcast(F32),
                                          bank[4][:, 0:D]).then_inc(sm["s_rx"], 1)
                i = s + 1
                if known(i):
                    dve.wait_ge(sm["s_ru"], i + 1)
                    dve.wait_ge(sm["s_rsil"], i + 1)
                    nc.vector.scalar_tensor_tensor(prod[:, q, 0:F], bank[2 * q + 1][:, 0:F], SA / (SH1 * SW),
                                                   sil[:, q, 0:F], ALU.mult, ALU.mult).then_inc(sm["s_rprod"], 1)
                    dve.wait_ge(sm["s_rhi"], i + 1)
                    nc.vector.tensor_tensor(ract[:, q, LO], prod[:, q, 0:F], ract[:, q, HI],
                                            ALU.subtract).then_inc(sm["s_rlo"], 1)

            dve.wait_ge(sm["s_ahi"], EARLY)
            run_tiles(dve, step, 2)
            shares1()

            t = 0
            for i in range(EARLY, B * ST):
                shared_dve(i)
                if i in DOWN:
                    accumulate(DOWN[i], range(TPB))
                    t = TPB
                elif TPB <= t < 2 * TPB:
                    combine(t)
                    combine(t + 1)
                    t += 2
            for t in range(t, NT):
                combine(t)
            accumulate(B - 1)

        @block.tensor
        def _(pe):
            def group(out_ap, terms, s=None):
                for i, (l, r) in enumerate(terms):
                    mm = nc.tensor.matmul(out_ap, l, r, start=(i == 0), stop=(i == len(terms) - 1))
                if s is not None:
                    mm.then_inc(sm[s], 1)
                return mm

            pe.wait_ge(sm["s_warm"], 1)
            for _ in range(WARM):
                nc.tensor.matmul(bank[0][:], warm[:, 0:P], warm[:], start=True, stop=True)

            for g in range(G):
                if g % 2 == 0:
                    pe.wait_ge(s_wc[g // 2], 16)
                for b in range(2):
                    if b == 1 or g < G2:
                        pe.wait_ge(sm["s_diag"], 2 * g + b + 1)
                        mm = nc.tensor.matmul(bank[6 + b][:], diag[:, b, g], wc_in[:, g], start=(g == 0),
                                              stop=(g == (G - 1 if b else G2 - 1)))
            mm.then_inc(sm["s_wbp"], 1)

            def project(layer, c):
                w = wbs if layer == 0 else wls
                for o in range(KT):
                    i = layer * B * KT + c * KT + o
                    if i >= 6:
                        pe.wait_ge(sm["s_hlo"], i - 5 if i < B * KT else i - 1)
                    group(h_bank(i)[:].rearrange("p (t n) -> p t n", n=P),
                          [(w[:, c, a, k, o * P:(o + 1) * P], xs[:, c * TPB:(c + 1) * TPB, b, k])
                           for k in range(KT) for a, b in PASSES], "s_h")

            def logits(layer, c):
                pe.wait_ge(sm["s_hlo"], (layer * B + c + 1) * KT)
                for t in range(c * TPB, (c + 1) * TPB):
                    mm = group(bank[6 + layer][:, t * E:(t + 1) * E],
                               [(hs[:, a, k, t * P:(t + 1) * P], rs[:, layer, b, k, :])
                                for k in range(KT) for a, b in PASSES])
                if c % 2 == 1:
                    mm.then_inc(sm["s_log"], 1)

            for c in range(B):
                pe.wait_ge(sm["s_xlo"], c + 1)
                pe.wait_ge(sm["s_wblo"], c + 1)
                project(0, c)
                if c == 1:
                    pe.wait_ge(sm["s_rsp"], 2)
                    pe.wait_ge(sm["s_wacc"], 3)
                if c == 1 or c == 2:
                    logits(0, c - 1)

            def lora(b):
                pe.wait_ge(sm["s_lbw"], b + 1)
                if b >= 1:
                    pe.wait_ge(sm["s_wlf"], b)
                for k in range(KT):
                    mm = nc.tensor.matmul(bank[7][:, k * D:(k + 1) * D], la[:, k * P:(k + 1) * P], lbw[:, b % 2],
                                          start=True, stop=True)
                mm.then_inc(sm["s_lora"], 1)

            def transposes(m):
                pe.wait_ge(sm["s_comb"], (m + 1) * 2 * E)
                if m == 0:
                    pe.wait_ge(sm["s_bias"], 2)
                    pe.wait_ge(sm["s_lg"], 2)
                else:
                    pe.wait_ge(sm["s_trlo"], m)
                for a in range(2):
                    for k in range(KT):
                        o = (a * KT + k) * P
                        mm = nc.tensor.transpose(bank[6][:, o:o + P], x1[:, 2 * m + a, k * P:(k + 1) * P], ident[:])
                mm.then_inc(sm["s_tr"], 1)

            def token_rows(c, tiles):
                for t in range(c * TPB + tiles[0], c * TPB + tiles[1] + 1):
                    if t >= c * TPB + 2:
                        pe.wait_ge(sm["s_rows"], t - 1)
                    for a in range(2):
                        for k in range(KT):
                            o = (a * KT + k) * P
                            mm = nc.tensor.transpose(bank16[4 + t % 2][:, o:o + P], hs[:, a, k, t * P:(t + 1) * P],
                                                     ident16[:])
                    mm.then_inc(sm["s_rt"], 1)

            def layer1_input(c):
                pe.wait_ge(sm["s_trlo"], (c + 1) * TPB // 2)
                pe.wait_ge(sm["s_wllo"], c + 1)
                if c >= 1:
                    pe.wait_ge(sm["s_rows"], c * TPB)
                project(1, c)

            for m in range(TWO):
                for j in range(PAIRS):
                    if m == 0:
                        pe.wait_ge(sm["s_w0lo"], j + 1)
                        if j < 2:
                            pe.wait_ge(sm["s_hlo"], (j + 2) * KT)
                    for a in range(2):
                        n = 2 * (m * PAIRS + j) + a
                        if n >= 4:
                            pe.wait_ge(sm["s_comb"], 2 * (n - a - 4) + 3 + a)
                        t = 2 * m + a
                        group(bank[n % 4][:], [(hs[:, x, k, t * P:(t + 1) * P], w0s[:, y, k, j * PW:(j + 1) * PW])
                                               for k in range(KT) for x, y in PASSES], "s_ffn")
                    if m < B and j == (m == 0):
                        lora(m)
                    if m == 0 and j in (1, 2):
                        if j == 1:
                            pe.wait_ge(sm["s_lg"], 1)
                        logits(0, j + 1)
                    if j == 1 and m >= 1:
                        transposes(m - 1)
                    if m >= 3 and m % 2 == 1:
                        c = (m - 3) // 2
                        if j == 0:
                            layer1_input(c)
                        if j == 2:
                            pe.wait_ge(sm["s_hlo"], (B + c + 1) * KT)
                            token_rows(c, (0, 1))
                        if j == 3:
                            if m == 3:
                                pe.wait_ge(sm["s_wlf"], B)
                            logits(1, c)
                            token_rows(c, (2, 3))

            def down(c, parts=(range(ST),)):
                for part in parts:
                    pe.wait_ge(sm["s_alo"], c * ST + part[-1] + 1)
                    for q in range(TPB):
                        if part[0] == 0:
                            if c == 0:
                                pe.wait_ge(sm["s_rows"], NT)
                                pe.wait_ge(sm["s_idx"], 1)
                            else:
                                pe.wait_ge(sm["s_acc"], (c - 1) * TPB + q + 1)
                        for f in part:
                            for n, (a, b) in enumerate(PASSES):
                                mm = nc.tensor.matmul(bank[4 + q][:, 0:D],
                                                      acts[0:SR[f], c % 2, f, a, q * P:(q + 1) * P], w_dn(b, f),
                                                      start=(f == 0 and n == 0), stop=(f == ST - 1 and n == 2))
                        if part[-1] == ST - 1:
                            mm.then_inc(sm["s_dn"], 1)

            def gate_up(i, between=None):
                c, f, p = i // ST, i % ST, side(i)
                if i == 0:
                    pe.wait_ge(sm["s_pclo"], -(-SHARED * WE // PIECE))
                if i >= 2:
                    pe.wait_ge(sm["s_prod"], i - 1)
                else:
                    pe.wait_ge(sm["s_comb"], NT * E - 4 + 4 * i)
                for g in range(2 if f < ST - 1 else 1):
                    if g and between is not None:
                        transposes(between)
                    mm = group(bank[2 * p + g][0:P if f < ST - 1 else 2 * REST],
                               [(w_gu(a, k, g, f), hs[:, b, k, c * S:(c + 1) * S])
                                for k in range(KT) for a, b in PASSES])
                mm.then_inc(sm["s_gu"], 1)

            def ranks():
                pe.wait_ge(sm["s_sel"], 1)
                sel = sel16[:].rearrange("p t e -> p (t e)")
                nc.tensor.matmul(bank[6][:, 0:NT * E], before[:], sel[:, NT * E:], start=True, stop=False)
                for d in range(1, NT):
                    nc.tensor.matmul(bank[6][:, 0:NT * E], ones16[:], sel[:, (NT - d) * E:(2 * NT - d) * E],
                                     start=False, stop=(d == NT - 1))
                for t in range(NT, 2 * NT):
                    mm = nc.tensor.matmul(bank[6][:, NT * E:NT * E + E], ones16[:], sel[:, t * E:(t + 1) * E],
                                          start=(t == NT), stop=(t == 2 * NT - 1))
                mm.then_inc(sm["s_rank"], 1)

            def experts(ap):
                return nc.values_load_multi_w_load_instructions(
                    ap, engines=(nc.tensor.engine,), min_val=SHARED * WE, max_val=(NEXP - 1) * WE,
                    skip_runtime_bounds_check_because="the table's entries are clamped where it is made")[1]

            for i in range(EARLY):
                if i == EARLY - 1:
                    pe.wait_ge(sm["s_idx"], 2)
                    places = experts(te[0:1, 0:5])
                gate_up(i, TWO - 1 if i == 0 else None)
                if i == 1:
                    layer1_input(B - 1)
                if i == 2:
                    logits(1, B - 1)
                if i == 3:
                    token_rows(B - 1, (0, 1))
                if i == 4:
                    token_rows(B - 1, (2, 3))
                    ranks()
                if i in DOWN:
                    down(DOWN[i])

            def step(s, par, down_at, gate_at):
                q = 1 - par
                i = s + 2
                if known(i):
                    pe.wait_ge(s_row[par], landed(i, par))
                    if isinstance(i, int) and i == 1:
                        pe.wait_ge(sm["s_rx"], i)
                    for a in range(2):
                        for k in range(KT):
                            o = (a * KT + k) * P
                            mm = nc.tensor.transpose(bank16[4][:, o:o + P], rows[:, par, o:o + P], ident16[:])
                    mm.then_inc(sm["s_ra"], 1)
                i = s - 1
                if known(i):
                    pe.wait_ge(sm["s_rcx"], i + 1)
                    if again(i):
                        pe.wait_ge(sm["s_ry"], i - 1)
                    group(bank[6 + q][:, 0:D],
                          [(aT[0:FS[f], q, f, a], w1s[0:FS[f], b, bass.ds(down_at + (KT * 2 * F + f * D), D)])
                           for f in range(FT) for a, b in PASSES], "s_rd")
                i = s
                if known(i):
                    pe.wait_ge(sm["s_rlo"], i + 1)
                    for f in range(FT):
                        for a in range(2):
                            o = (2 * f + a) * P
                            mm = nc.tensor.transpose(bank16[5][0:FS[f], o:o + P],
                                                     ract[:, par, a, f * P:f * P + FS[f]], ident16[:])
                    mm.then_inc(sm["s_rc"], 1)
                i = s + 2
                if known(i):
                    pe.wait_ge(sm["s_rx"], i + 1)
                    for g, done in enumerate(("s_rg", "s_ru")):
                        group(bank[2 * par + g][:, 0:F],
                              [(rT[:, par, a, k], w1s[:, b, bass.ds(gate_at + (k * 2 + g) * F, F)])
                               for k in range(KT) for a, b in PASSES], done)

            pe.wait_ge(sm["s_acc"], TPB + 1)
            for s in range(-2, 3):
                step(s, s % 2, places[s - 1] if s >= 1 else None, places[s + 2])
            with pe.Fori(0, LOOPS) as j:
                a, b, c, d = experts(te4[0:1, bass.ds(j, 1), :].rearrange("p a b -> p (a b)"))
                step(j * 2 + 3, 1, a, c)
                step(j * 2 + 4, 0, b, d)
            places = experts(te[0:1, TILES - 3:TILES])
            for s in range(3 + 2 * LOOPS, TILES + 1):
                step(s, s % 2, places[s - 1 - (TILES - 3)], None)
                if s == TILES - 2:
                    gate_up(EARLY)

            pe.wait_ge(sm["s_rcx"], TILES)
            for i in range(EARLY, B * ST):
                if i > EARLY:
                    if i == EARLY + 1:
                        pe.wait_ge(sm["s_rprod"], TILES)
                    gate_up(i)
                if i in DOWN:
                    pe.wait_ge(sm["s_ry"], TILES)
                    down(DOWN[i])
            down(B - 1, (range(ST - 2), range(ST - 2, ST)))


def kernel(x, cond_8, L0_cond_weight, L0_cond_mask, L0_cond_bias, L0_ffn_router_w, L0_ffn_expert_weights,
           L1_cond_W_base, L1_cond_b_base, L1_cond_As, L1_cond_Bs, L1_ffn_gate_w, L1_ffn_exp_gate,
           L1_ffn_exp_up, L1_ffn_exp_down, L1_ffn_sh_gate, L1_ffn_sh_up, L1_ffn_sh_down):
    import numpy as np
    import concourse.bacc as bacc
    from concourse.bass_utils import run_bass_kernel_spmd

    Bb, S, D = x.shape
    N, KT = Bb * S, D // P
    E, R, _ = L1_cond_As.shape
    F = L1_ffn_exp_gate.shape[2]

    def by_k(a):
        return np.ascontiguousarray(a.reshape(KT, P, -1).transpose(1, 0, 2))

    def swiglu_rows(wg, wu, wd):
        n = wg.shape[0]
        gu = np.concatenate([wg, wu], axis=2).reshape(n, KT, P, 2 * F).transpose(2, 0, 1, 3).reshape(P, n, -1)
        ft = -(-F // P)
        dn = np.zeros((n, ft * P, D), wd.dtype)
        dn[:, :F] = wd
        dn = dn.reshape(n, ft, P, D).transpose(2, 0, 1, 3).reshape(P, n, -1)
        return np.concatenate([gu, dn], axis=2)

    def side_by_side(wg, wu, wd):
        g, u = (w.transpose(1, 0, 2).reshape(D, -1) for w in (wg, wu))
        full = g.shape[1] // P * P
        gu = np.concatenate([g[:, :full], u[:, :full], u[:, full:], g[:, full:]], axis=1)
        dn = np.zeros((full + P, D), wd.dtype)
        dn[:g.shape[1]] = wd.reshape(-1, D)
        return np.concatenate([w.reshape(-1, P, w.shape[1]).transpose(1, 0, 2).reshape(P, -1)
                               for w in (gu, dn)], axis=1)

    x = np.asarray(x)
    tok = x.reshape(N, D)
    c = np.asarray
    shared = side_by_side(c(L1_ffn_sh_gate), c(L1_ffn_sh_up), c(L1_ffn_sh_down))
    routed = swiglu_rows(c(L1_ffn_exp_gate), c(L1_ffn_exp_up), c(L1_ffn_exp_down)).reshape(P, -1)
    ins = {
        "cond_row": c(cond_8).reshape(1, -1),
        "cond_er": np.ascontiguousarray(np.repeat(c(cond_8).T, R, axis=0)),
        "xT": by_k(tok.T),
        "x": np.ascontiguousarray(tok.reshape(N // P, P, D).transpose(1, 0, 2)),
        "wc": np.ascontiguousarray(c(L0_cond_weight).reshape(E, D, KT, P).transpose(3, 0, 2, 1).reshape(P, E, KT * D)),
        "mask": by_k(c(L0_cond_mask).T).reshape(P, KT * D),
        "bias0": np.ascontiguousarray(c(L0_cond_bias).reshape(KT, P).T),
        "router": by_k(c(L0_ffn_router_w).T),
        "w0": by_k(c(L0_ffn_expert_weights).transpose(1, 0, 2).reshape(D, E * D)),
        "wbase": by_k(c(L1_cond_W_base).T).reshape(P, KT * D),
        "bias1": np.ascontiguousarray(c(L1_cond_b_base).reshape(KT, P).T),
        "lora_a": c(L1_cond_As).reshape(E * R, D),
        "lora_b": np.ascontiguousarray(c(L1_cond_Bs).transpose(0, 2, 1).reshape(E * R, D)),
        "gate": by_k(c(L1_ffn_gate_w)),
        "w1": np.ascontiguousarray(np.concatenate([shared, routed], axis=1).reshape(P, -1, routed.shape[1] // E)),
    }
    nc = bacc.Bacc("TRN2", target_bir_lowering=False, num_devices=1)
    aps = {n: nc.dram_tensor(n, a.shape, mybir.dt.from_np(a.dtype), kind="ExternalInput").ap()
           for n, a in ins.items()}
    out = nc.dram_tensor("out", (P, N // P, D), F32, kind="ExternalOutput").ap()
    build_program(nc, out=out, **aps)
    r = run_bass_kernel_spmd(nc, [ins], core_ids=[0])
    return r.results[0]["out"].reshape(P, N // P, D).transpose(1, 0, 2).reshape(Bb, S, D)
```
